# Optimizing a Trainium2 kernel written in Bass

```python
import numpy as np
import jax
import jax.numpy as jnp

def _softmax(x, axis=-1):
    return jax.nn.softmax(x, axis=axis)

def _gelu(x):
    return jax.nn.gelu(x, approximate=True)

def _silu(x):
    return jax.nn.silu(x)

def _sigmoid(x):
    return jax.nn.sigmoid(x)

def _layernorm(x, axis=-1, eps=1e-05):
    m = jnp.mean(x, axis=axis, keepdims=True)
    v = jnp.var(x, axis=axis, keepdims=True)
    return (x - m) / jnp.sqrt(v + eps)

def _scatter_add(tgt, idx, src, axis=0):
    return tgt.at[idx].add(src)

def _segment_sum(src, seg, n):
    return jax.ops.segment_sum(src, seg, n)
kernel_name = 'mk_macaron_d1_jaxref_r8_b293f8'

def setup_inputs(seed: int=0):
    np.random.seed(seed)
    _w = jnp.asarray

    def _L0_attn_setup():
        import math
        import jax, jax.numpy as jnp
        import numpy as np
        HIDDEN = 128
        HEADS = 16
        HEAD_DIM = HIDDEN // HEADS
        SEQ = 512
        PATCH = 508
        EPS = 1e-06

        def _rms_norm(t, w):
            return t * jax.lax.rsqrt(jnp.mean(t * t, axis=-1, keepdims=True) + EPS) * w

        def _apply_rope(t, cos, sin):
            b, s, h, d = t.shape
            P = cos.shape[0]
            tail = t[:, s - P:].reshape(b, P, h, d // 2, 2)
            x0, x1 = (tail[..., 0], tail[..., 1])
            c = cos[None, :, None, :]
            sn = sin[None, :, None, :]
            rot = jnp.stack([x0 * c - x1 * sn, x0 * sn + x1 * c], axis=-1).reshape(b, P, h, d)
            return jnp.concatenate([t[:, :s - P], rot], axis=1)
        key = jax.random.key(seed)
        ks = jax.random.split(key, 8)
        return {'x': jax.random.normal(ks[0], (1, SEQ, HIDDEN), dtype=jnp.float32), 'rope_cos': jax.random.uniform(ks[1], (PATCH, HEAD_DIM // 2), dtype=jnp.float32), 'rope_sin': jax.random.uniform(ks[2], (PATCH, HEAD_DIM // 2), dtype=jnp.float32), 'wq': jax.random.normal(ks[3], (HIDDEN, HIDDEN), dtype=jnp.float32) / math.sqrt(HIDDEN), 'wk': jax.random.normal(ks[4], (HIDDEN, HIDDEN), dtype=jnp.float32) / math.sqrt(HIDDEN), 'wv': jax.random.normal(ks[5], (HIDDEN, HIDDEN), dtype=jnp.float32) / math.sqrt(HIDDEN), 'wo': jax.random.normal(ks[6], (HIDDEN, HIDDEN), dtype=jnp.float32) / math.sqrt(HIDDEN), 'q_norm_w': jnp.ones((HEAD_DIM,), dtype=jnp.float32), 'k_norm_w': jnp.ones((HEAD_DIM,), dtype=jnp.float32)}
    _L0_attn_in = _L0_attn_setup()

    def _L0_ffn_setup():
        import jax, jax.numpy as jnp
        import numpy as np
        B, S, H = (2, 512, 128)
        E, K, I = (8, 2, 176)
        key = jax.random.key(seed)
        ks = jax.random.split(key, 9)
        sc = 0.02
        return {'hidden_states': jax.random.normal(ks[0], (B, S, H), jnp.float32), 'gate_w': jax.random.normal(ks[1], (E, H), jnp.float32) * sc, 'w_gate': jax.random.normal(ks[2], (E, H, I), jnp.float32) * sc, 'w_up': jax.random.normal(ks[3], (E, H, I), jnp.float32) * sc, 'w_down': jax.random.normal(ks[4], (E, I, H), jnp.float32) * sc, 'sw_gate': jax.random.normal(ks[5], (H, I), jnp.float32) * sc, 'sw_up': jax.random.normal(ks[6], (H, I), jnp.float32) * sc, 'sw_down': jax.random.normal(ks[7], (I, H), jnp.float32) * sc, 'shared_gate_w': jax.random.normal(ks[8], (1, H), jnp.float32) * sc}
    _L0_ffn_in = _L0_ffn_setup()
    _d = {'L0_attn_x': _L0_attn_in['x'], 'L0_attn_rope_cos': _L0_attn_in['rope_cos'], 'L0_attn_rope_sin': _L0_attn_in['rope_sin'], 'L0_attn_wq': _L0_attn_in['wq'], 'L0_attn_wk': _L0_attn_in['wk'], 'L0_attn_wv': _L0_attn_in['wv'], 'L0_attn_wo': _L0_attn_in['wo'], 'L0_attn_q_norm_w': _L0_attn_in['q_norm_w'], 'L0_attn_k_norm_w': _L0_attn_in['k_norm_w'], 'L0_ffn_gate_w': _L0_ffn_in['gate_w'], 'L0_ffn_w_gate': _L0_ffn_in['w_gate'], 'L0_ffn_w_up': _L0_ffn_in['w_up'], 'L0_ffn_w_down': _L0_ffn_in['w_down'], 'L0_ffn_sw_gate': _L0_ffn_in['sw_gate'], 'L0_ffn_sw_up': _L0_ffn_in['sw_up'], 'L0_ffn_sw_down': _L0_ffn_in['sw_down'], 'L0_ffn_shared_gate_w': _L0_ffn_in['shared_gate_w']}
    _x0 = _d['L0_attn_x']
    _d['L0_attn_x'] = jax.random.normal(jax.random.fold_in(jax.random.key(seed), 1), (2, 2048, 128), dtype=_x0.dtype)
    del _x0
    return _d

def reference(L0_attn_x, L0_attn_rope_cos, L0_attn_rope_sin, L0_attn_wq, L0_attn_wk, L0_attn_wv, L0_attn_wo, L0_attn_q_norm_w, L0_attn_k_norm_w, L0_ffn_gate_w, L0_ffn_w_gate, L0_ffn_w_up, L0_ffn_w_down, L0_ffn_sw_gate, L0_ffn_sw_up, L0_ffn_sw_down, L0_ffn_shared_gate_w):

    def _L0_attn_ref(x, rope_cos, rope_sin, wq, wk, wv, wo, q_norm_w, k_norm_w):
        import math
        import jax, jax.numpy as jnp
        import numpy as np
        HIDDEN = 128
        HEADS = 16
        HEAD_DIM = HIDDEN // HEADS
        SEQ = 512
        PATCH = 508
        EPS = 1e-06

        def _rms_norm(t, w):
            return t * jax.lax.rsqrt(jnp.mean(t * t, axis=-1, keepdims=True) + EPS) * w

        def _apply_rope(t, cos, sin):
            b, s, h, d = t.shape
            P = cos.shape[0]
            tail = t[:, s - P:].reshape(b, P, h, d // 2, 2)
            x0, x1 = (tail[..., 0], tail[..., 1])
            c = cos[None, :, None, :]
            sn = sin[None, :, None, :]
            rot = jnp.stack([x0 * c - x1 * sn, x0 * sn + x1 * c], axis=-1).reshape(b, P, h, d)
            return jnp.concatenate([t[:, :s - P], rot], axis=1)
        b, s, _ = x.shape
        q = (x @ wq.T).reshape(b, s, HEADS, HEAD_DIM)
        k = (x @ wk.T).reshape(b, s, HEADS, HEAD_DIM)
        v = (x @ wv.T).reshape(b, s, HEADS, HEAD_DIM)
        q = _rms_norm(q, q_norm_w)
        k = _rms_norm(k, k_norm_w)
        q = _apply_rope(q, rope_cos, rope_sin)
        k = _apply_rope(k, rope_cos, rope_sin)
        q = q / math.sqrt(HEAD_DIM)
        scores = jnp.einsum('bqhd,bkhd->bhqk', q, k)
        attn = jax.nn.softmax(scores.astype(jnp.float32), axis=-1)
        out = jnp.einsum('bhqk,bkhd->bqhd', attn, v).reshape(b, s, HIDDEN)
        return out @ wo.T

    def _L0_ffn_ref(hidden_states, gate_w, w_gate, w_up, w_down, sw_gate, sw_up, sw_down, shared_gate_w):
        import jax, jax.numpy as jnp
        import numpy as np
        B, S, H = (2, 512, 128)
        E, K, I = (8, 2, 176)
        b, s, h = hidden_states.shape
        x = hidden_states.reshape(-1, h)
        logits = jnp.einsum('th,eh->te', x, gate_w)
        probs = jax.nn.softmax(logits.astype(jnp.float32), axis=-1)
        topk_w, topk_i = jax.lax.top_k(probs, K)
        topk_w = topk_w / jnp.sum(topk_w, axis=-1, keepdims=True)
        combine = jnp.sum(jax.nn.one_hot(topk_i, E, dtype=topk_w.dtype) * topk_w[..., None], axis=1)
        combine = combine.astype(x.dtype)
        g = jnp.einsum('th,ehi->eti', x, w_gate)
        u = jnp.einsum('th,ehi->eti', x, w_up)
        eo = jnp.einsum('eti,eih->eth', jax.nn.silu(g) * u, w_down)
        out = jnp.einsum('te,eth->th', combine, eo)
        sg = jax.nn.sigmoid(jnp.einsum('th,oh->to', x, shared_gate_w))
        so = jax.nn.silu(x @ sw_gate) * (x @ sw_up) @ sw_down
        out = out + sg * so
        return out.reshape(b, s, h)
    x = L0_attn_x
    x = x + 0.5 * _L0_ffn_ref(_layernorm(x, axis=-1), L0_ffn_gate_w, L0_ffn_w_gate, L0_ffn_w_up, L0_ffn_w_down, L0_ffn_sw_gate, L0_ffn_sw_up, L0_ffn_sw_down, L0_ffn_shared_gate_w)
    x = x + _L0_attn_ref(_layernorm(x, axis=-1), L0_attn_rope_cos, L0_attn_rope_sin, L0_attn_wq, L0_attn_wk, L0_attn_wv, L0_attn_wo, L0_attn_q_norm_w, L0_attn_k_norm_w)
    x = x + 0.5 * _L0_ffn_ref(_layernorm(x, axis=-1), L0_ffn_gate_w, L0_ffn_w_gate, L0_ffn_w_up, L0_ffn_w_down, L0_ffn_sw_gate, L0_ffn_sw_up, L0_ffn_sw_down, L0_ffn_shared_gate_w)
    return x

_drawn_inputs = setup_inputs


def setup_inputs(seed=0):
    import zlib

    import numpy as np

    out = dict(_drawn_inputs(seed))
    spreads = {'L0_attn_q_norm_w': (1.0, 0.6), 'L0_attn_k_norm_w': (1.0, 0.6)}
    factors = {'L0_attn_rope_cos': 5.297,
     'L0_attn_rope_sin': 5.18,
     'L0_ffn_gate_w': 8.0,
     'L0_ffn_w_gate': 8.0,
     'L0_ffn_w_up': 8.0,
     'L0_ffn_w_down': 8.0,
     'L0_ffn_sw_gate': 8.0,
     'L0_ffn_sw_up': 8.0,
     'L0_ffn_sw_down': 8.0,
     'L0_ffn_shared_gate_w': 8.0}
    for name, (base, spread) in spreads.items():
        noise = np.random.default_rng([zlib.crc32(name.encode()), seed]).standard_normal(out[name].shape)
        drawn = base * np.exp(spread * noise) if base else spread * noise
        out[name] = jnp.asarray(drawn.astype(out[name].dtype))
    for name, factor in factors.items():
        out[name] = (out[name] * factor).astype(out[name].dtype)
    return out
```

```python
from contextlib import ExitStack

import concourse.bass as bass
from concourse import mybir

F32 = mybir.dt.float32
BF16 = mybir.dt.bfloat16
ALU = mybir.AluOpType
ACT = mybir.ActivationFunctionType
AX = mybir.AxisListType

P = 128
D = 128
BATCH, SEQ = 2, 2048
T = BATCH * SEQ
NT = T // P
BLK = 512
NB = T // BLK
TPB = BLK // P
BPS = SEQ // BLK
E = 8
I = 176
R = (E + 1) * I
CH = -(-R // P)
HEADS, HD = 16, 8
HD1 = HD + 1
BH = BATCH * HEADS
PATCH = 508
KT = SEQ // P
LN_EPS, RMS_EPS = 1e-5, 1e-6
BUFS = 3
PROBS = 4
PRIME = 1

PAIRS = [(0, 0), (0, 1), (0, 2), (1, 0), (1, 1), (2, 0)]
KR = len(PAIRS) * HD
MR = 3
MROW = 96


def prime(eng, *sems):
    for s in sems:
        eng.sem_inc(s, PRIME)


def build(nc, x_in, rope_cos, rope_sin, wq, wk, wv, wo, q_norm_w, k_norm_w, gate_w, w_gate, w_up,
          w_down, sw_gate, sw_up, sw_down, shared_gate_w, c_ident, c_expert_rows, c_head_rows,
          c_dim_rows, c_pair_rows, c_head_mean, c_swap, c_rank, out):
    x_dram = x_in.rearrange("b (n p) d -> p (b n) d", p=P)
    out_dram = out.rearrange("b (n p) d -> p (b n) d", p=P)
    q_rows = nc.dram_tensor("q_rows", (BH, KR, SEQ), BF16).ap()
    k_rows = nc.dram_tensor("k_rows", (BH, KR, SEQ), BF16).ap()
    o_rows = nc.dram_tensor("o_rows", (BH, HD, SEQ), F32).ap()
    den_rows = nc.dram_tensor("den_rows", (BH, 1, SEQ), F32).ap()

    nc.disable_value_cache = True
    with ExitStack() as ctx:
        def sb(name, shape, dt=F32):
            return ctx.enter_context(nc.sbuf_tensor(name, shape, dt))

        def sem(name):
            return ctx.enter_context(nc.semaphore(name))

        ps = ctx.enter_context(nc.psum_tensor("ps", [P, 8, BLK], F32))

        x = sb("x", [P, NT, D])
        xnT = sb("xnT", [P, T])
        wgate = sb("wgate", [P, CH * P])
        wup = sb("wup", [P, CH * P])
        wdown = sb("wdown", [P, CH, D])
        ident = sb("ident", [P, P])
        identb = sb("identb", [P, P], BF16)
        expert_rows = sb("expert_rows", [3 * (E + 1), CH * P], BF16)
        head_rows = sb("head_rows", [HEADS, P])
        head_mean = sb("head_mean", [P, P])
        swap = sb("swap", [P, P])
        rank = sb("rank", [P, E])
        gateT = sb("gateT", [P, E + 1])
        wqT = sb("wqT", [P, D])
        wkT = sb("wkT", [P, D])
        wvT = sb("wvT", [P, D])
        woT = sb("woT", [P, D])
        norm_w = sb("norm_w", [P, 2])
        rope = sb("rope", [P, 2, BLK])
        logits = sb("logits", [P, NT, E + 1])
        combT = sb("combT", [3 * (E + 1), T], BF16)
        v = sb("v", [P, BATCH, HEADS, KT, HD])
        work = sb("work", [P, max(CH, PROBS * BPS) * BLK])
        q_head = [sb(f"q_head{i}", [P, SEQ], BF16) for i in range(BUFS)]
        k_head = [sb(f"k_head{i}", [P, SEQ], BF16) for i in range(BUFS)]
        vals = [sb(f"vals{i}", [P, KT, 32]) for i in range(BUFS)]

        load_phase(nc, sem, sb, locals())
        norm_phase(nc, sem, "n1", ps, x, xnT, ident, gateT, logits)
        routing_phase(nc, sem, "r1", ps, logits, rank, identb, combT)
        expert_phase(nc, sem, "e1", ps, x, xnT, wgate, wup, wdown, expert_rows, combT, ident, work,
                     None, (q_head, k_head, vals))
        norm_phase(nc, sem, "n2", ps, x, xnT, ident, None, None)
        qkv_phase(nc, sem, ps, xnT, (wqT, wkT, wvT), norm_w, head_mean, swap, rope, ident, v,
                  q_rows, k_rows)
        attention_phase(nc, sem, ps, v, identb, work, q_head, k_head, vals, q_rows, k_rows, o_rows,
                        den_rows)
        output_phase(nc, sem, ps, x, woT, head_rows, o_rows, den_rows)
        norm_phase(nc, sem, "n3", ps, x, xnT, ident, gateT, logits)
        routing_phase(nc, sem, "r3", ps, logits, rank, identb, combT)
        expert_phase(nc, sem, "e3", ps, x, xnT, wgate, wup, wdown, expert_rows, combT, ident, work,
                     out_dram)


def load_phase(nc, sem, sb, g):
    ps, ident = g["ps"], g["ident"]
    loaded = sem("ld_loaded")
    consts = sem("ld_consts")
    filled = sem("ld_filled")
    turned = sem("ld_turned")
    copied = sem("ld_copied")
    with ExitStack() as tmp:
        def tb(name, shape, dt=F32):
            return tmp.enter_context(nc.sbuf_tensor(name, shape, dt))
        raw = tb("ld_raw", [P, 4, D])
        raw_gate = tb("ld_gate", [E + 1, D])
        raw_rope = tb("ld_rope", [P, 2, TPB, HD // 2])
        ropeT = tb("ld_ropeT", [HD // 2, 2, BLK])
        rows32 = tb("ld_rows32", [3 * (E + 1), CH * P])
        dim_rows = tb("ld_dim_rows", [HD, P])
        pair_rows = tb("ld_pair_rows", [HD // 2, 2, P])
        raw_nw = tb("ld_nw", [HD, 2])
        first_turned = P - (PATCH - (TPB - 1) * P)
        block = tmp.enter_context(nc.Block())

        @block.sync
        def _(sp):
            sp.dma_start(ident[:], g["c_ident"]).then_inc(consts, 16)
            for i, w in enumerate(("wq", "wk", "wv", "wo")):
                sp.dma_start(raw[:, i, :], g[w]).then_inc(consts, 16)
            sp.dma_start(raw_gate[0:E, :], g["gate_w"]).then_inc(consts, 16)
            sp.dma_start(raw_gate[E:E + 1, :], g["shared_gate_w"]).then_inc(consts, 16)
            sp.dma_start(dim_rows[:], g["c_dim_rows"]).then_inc(consts, 16)
            sp.dma_start(pair_rows[:], g["c_pair_rows"]).then_inc(consts, 16)
            sp.dma_start(raw_nw[:, 0:1], g["q_norm_w"].rearrange("(d a) -> d a", a=1)).then_inc(consts, 16)
            sp.dma_start(raw_nw[:, 1:2], g["k_norm_w"].rearrange("(d a) -> d a", a=1)).then_inc(consts, 16)
            sp.dma_start(rows32[:], g["c_expert_rows"]).then_inc(consts, 16)
            sp.wait_ge(filled, 2)
            for i, t in enumerate(("rope_cos", "rope_sin")):
                head = P - first_turned
                sp.dma_start(raw_rope[first_turned:P, i, 0, :], g[t][0:head, :]).then_inc(consts, 16)
                sp.dma_start(raw_rope[:, i, 1:TPB, :],
                             g[t][head:PATCH, :].rearrange("(n p) d -> p n d", p=P)).then_inc(consts, 16)
            sp.wait_ge(consts, 16 * 16)
            sp.wait_ge(loaded, 16 * 15)

        @block.gpsimd
        def _(pool):
            n = NT // 4
            for i in range(4):
                pool.dma_start(g["x"][:, i * n:(i + 1) * n, :], g["x_dram"][:, i * n:(i + 1) * n, :]).then_inc(loaded, 16)
            pool.dma_start(g["wgate"][:, 0:E * I].rearrange("h (e i) -> h e i", e=E),
                           g["w_gate"].rearrange("e h i -> h e i")).then_inc(loaded, 16)
            pool.dma_start(g["wgate"][:, E * I:R], g["sw_gate"]).then_inc(loaded, 16)
            pool.dma_start(g["wup"][:, 0:E * I].rearrange("h (e i) -> h e i", e=E),
                           g["w_up"].rearrange("e h i -> h e i")).then_inc(loaded, 16)
            pool.dma_start(g["wup"][:, E * I:R], g["sw_up"]).then_inc(loaded, 16)
            full = E * I // P
            assert full * P == E * I and (CH - full - 1) * P < I <= (CH - full) * P
            pool.dma_start(g["wdown"][:, 0:full, :],
                           g["w_down"].rearrange("e i h -> (e i) h").rearrange("(c p) h -> p c h", p=P)).then_inc(loaded, 16)
            pool.dma_start(g["wdown"][:, full, :], g["sw_down"][0:P, :]).then_inc(loaded, 16)
            pool.dma_start(g["wdown"][0:I - P, full + 1, :], g["sw_down"][P:I, :]).then_inc(loaded, 16)
            pool.dma_start(g["head_rows"][:], g["c_head_rows"]).then_inc(loaded, 16)
            pool.dma_start(g["head_mean"][:], g["c_head_mean"]).then_inc(loaded, 16)
            pool.dma_start(g["swap"][:], g["c_swap"]).then_inc(loaded, 16)
            pool.dma_start(g["rank"][:], g["c_rank"]).then_inc(loaded, 16)

        @block.tensor
        def _(pe):
            pe.wait_ge(consts, 16 * 16)
            for i in range(4):
                pe.transpose(ps[:, i, 0:D], raw[:, i, :], ident[:]).then_inc(turned, 1)
            pe.transpose(ps[:, 4, 0:E + 1], raw_gate[:], ident[0:E + 1, 0:E + 1]).then_inc(turned, 1)
            pe.matmul(ps[:, 5, 0:2], dim_rows[:], raw_nw[:], start=True, stop=True).then_inc(turned, 1)
            for i in range(2):
                for n in range(TPB):
                    last = pe.transpose(ps[0:HD // 2, 6 + i, n * P:(n + 1) * P], raw_rope[:, i, n, :], ident[:])
                last.then_inc(turned, 1)
            for i in range(2):
                pe.wait_ge(copied, 7 + i)
                pe.matmul(ps[:, i, :], pair_rows[:, i, :], ropeT[:, i, :], start=True, stop=True).then_inc(turned, 1)

        @block.vector
        def _(dve):
            dve.memset(g["wgate"][:, R:], 0.0)
            dve.memset(g["wup"][:, R:], 0.0)
            dve.memset(raw_rope[:, 0, :, :], 1.0).then_inc(filled, 1)
            dve.memset(raw_rope[:, 1, :, :], 0.0).then_inc(filled, 1)
            dve.wait_ge(turned, 6)
            for i, w in enumerate(("wqT", "wkT", "wvT", "woT")):
                dve.tensor_copy(g[w][:], ps[:, i, 0:D]).then_inc(copied, 1)
            dve.tensor_copy(g["gateT"][:], ps[:, 4, 0:E + 1]).then_inc(copied, 1)
            dve.tensor_scalar(g["norm_w"][:, 0:1], ps[:, 5, 0:1], float(HD) ** -0.5, None, ALU.mult).then_inc(copied, 1)
            for i in range(2):
                dve.wait_ge(turned, 7 + i)
                dve.tensor_copy(ropeT[:, i, :], ps[0:HD // 2, 6 + i, :]).then_inc(copied, 1)
            dve.tensor_copy(g["norm_w"][:, 1:2], ps[:, 5, 1:2])
            dve.tensor_copy(g["identb"][:], ident[:])
            dve.tensor_copy(g["expert_rows"][:], rows32[:])
            for i in range(2):
                dve.wait_ge(turned, 9 + i)
                dve.tensor_copy(g["rope"][:, i, :], ps[:, i, :])


def norm_phase(nc, sem, tag, ps, x, xnT, ident, gateT, logits):
    made = sem(tag + "_made")
    turned = [sem(f"{tag}_turned{i}") for i in range(2)]
    kept = [sem(f"{tag}_kept{i}") for i in range(2)]
    scored = sem(tag + "_scored")
    scored_kept = sem(tag + "_scored_kept")
    back = sem(tag + "_back")
    back_kept = sem(tag + "_back_kept")
    rooted = sem(tag + "_rooted")
    STEPS = 2 * TPB + 8
    with ExitStack() as tmp:
        stats = tmp.enter_context(nc.sbuf_tensor(tag + "_stats", [P, 2, TPB, 6], F32))
        tmp3 = tmp.enter_context(nc.sbuf_tensor(tag + "_tmp3", [P, 2, 3, TPB], F32))
        mean = tmp.enter_context(nc.sbuf_tensor(tag + "_mean", [P, 2, TPB], F32))
        std = tmp.enter_context(nc.sbuf_tensor(tag + "_std", [P, 2, TPB], F32))
        rstd = tmp.enter_context(nc.sbuf_tensor(tag + "_rstd", [P, 2, TPB], F32))
        xn = tmp.enter_context(nc.sbuf_tensor(tag + "_xn", [P, 2, TPB, D], F32))
        lgT = tmp.enter_context(nc.sbuf_tensor(tag + "_lgT", [E + 1, BLK], F32))
        block = tmp.enter_context(nc.Block())

        @block.vector
        def _(dve):
            with dve.Fori(0, NB // 2) as it:
                for par in range(2):
                    blk = it * 2 + par
                    for j in range(TPB):
                        dve.bn_stats(stats[:, par, j, :], x[:, blk * TPB + j, :]).then_inc(made, 1)
                    even, odd = stats[:, par, :, 0:3], stats[:, par, :, 3:6]
                    dve.wait_ge(made, blk * STEPS + TPB)
                    dve.tensor_tensor(tmp3[:, par, 0, :], even[:, :, 1], odd[:, :, 1], ALU.add).then_inc(made, 1)
                    dve.tensor_tensor(tmp3[:, par, 1, :], even[:, :, 1], odd[:, :, 1], ALU.subtract).then_inc(made, 1)
                    dve.tensor_tensor(tmp3[:, par, 2, :], even[:, :, 2], odd[:, :, 2], ALU.add).then_inc(made, 1)
                    dve.wait_ge(made, blk * STEPS + TPB + 3)
                    dve.tensor_scalar(mean[:, par, :], tmp3[:, par, 0, :], 0.5, None, ALU.mult).then_inc(made, 1)
                    dve.scalar_tensor_tensor(tmp3[:, par, 1, :], tmp3[:, par, 1, :], 0.25, tmp3[:, par, 1, :],
                                             ALU.mult, ALU.mult).then_inc(made, 1)
                    dve.tensor_scalar(tmp3[:, par, 2, :], tmp3[:, par, 2, :], 1.0 / D, LN_EPS, ALU.mult,
                                      ALU.add).then_inc(made, 1)
                    dve.wait_ge(made, blk * STEPS + TPB + 6)
                    dve.tensor_tensor(std[:, par, :], tmp3[:, par, 1, :], tmp3[:, par, 2, :], ALU.add).then_inc(made, 1)
                    dve.wait_ge(rooted, blk + 1)
                    dve.reciprocal(rstd[:, par, :], std[:, par, :]).then_inc(made, 1)
                    dve.wait_ge(made, blk * STEPS + TPB + 8)
                    dve.wait_ge(turned[par], it + PRIME)
                    for j in range(TPB):
                        dve.tensor_scalar(xn[:, par, j, :], x[:, blk * TPB + j, :], mean[:, par, j:j + 1],
                                          rstd[:, par, j:j + 1], ALU.subtract, ALU.mult).then_inc(made, 1)

        @block.tensor
        def _(pe):
            prime(pe, *turned)
            with pe.Fori(0, NB // 2) as it:
                for par in range(2):
                    blk = it * 2 + par
                    pe.wait_ge(made, blk * STEPS + STEPS)
                    pe.wait_ge(kept[par], it + PRIME)
                    for j in range(TPB):
                        last = pe.transpose(ps[:, par, j * P:(j + 1) * P], xn[:, par, j, :], ident[:])
                    last.then_inc(turned[par], 1)
                    if gateT is None:
                        continue
                    pe.wait_ge(kept[par], it + 1 + PRIME)
                    pe.matmul(ps[0:E + 1, 2, :], gateT[:], xnT[:, bass.ds(blk * BLK, BLK)],
                              start=True, stop=True).then_inc(scored, 1)
                    pe.wait_ge(scored_kept, blk + 1)
                    for j in range(TPB):
                        last = pe.matmul(ps[:, 3, j * (E + 1):(j + 1) * (E + 1)], lgT[:, j * P:(j + 1) * P],
                                         ident[0:E + 1, 0:E + 1], start=True, stop=True)
                    last.then_inc(back, 1)

        @block.scalar
        def _(act):
            prime(act, *kept)
            with act.Fori(0, NB // 2) as it:
                for par in range(2):
                    blk = it * 2 + par
                    act.wait_ge(made, blk * STEPS + TPB + 7)
                    act.activation(std[:, par, :], std[:, par, :], ACT.Sqrt).then_inc(rooted, 1)
                    act.wait_ge(turned[par], it + 1 + PRIME)
                    act.activation(xnT[:, bass.ds(blk * BLK, BLK)], ps[:, par, :], ACT.Copy).then_inc(kept[par], 1)
                    if gateT is None:
                        continue
                    act.wait_ge(scored, blk + 1)
                    act.activation(lgT[:], ps[0:E + 1, 2, :], ACT.Copy).then_inc(scored_kept, 1)
                    act.wait_ge(back, blk + 1)
                    act.activation(logits[:, bass.ds(blk * TPB, TPB), :],
                                   ps[:, 3, 0:TPB * (E + 1)].rearrange("p (n e) -> p n e", e=E + 1),
                                   ACT.Copy).then_inc(back_kept, 1)


def routing_phase(nc, sem, tag, ps, logits, rank, identb, combT):
    step = sem(tag + "_step")
    shifted = sem(tag + "_shifted")
    exped = sem(tag + "_exped")
    split = sem(tag + "_split")
    turned = sem(tag + "_turned")
    kept = sem(tag + "_kept")
    NE = E + 1
    with ExitStack() as tmp:
        def tb(name, shape, dt=F32):
            return tmp.enter_context(nc.sbuf_tensor(f"{tag}_{name}", shape, dt))
        ex = tb("ex", [P, NT, E])
        ex9 = tb("ex9", [P, NT, 1])
        prob = tb("prob", [P, NT, E])
        key = tb("key", [P, NT, E])
        first = tb("first", [P, NT, E])
        both = tb("both", [P, NT, E])
        rest = tb("rest", [P, NT, E])
        top = tb("top", [P, 6, NT])
        comb = tb("comb", [P, NT, NE])
        resid = tb("resid", [P, NT, NE])
        parts = tb("parts", [P, NT, 3, NE], BF16)
        block = tmp.enter_context(nc.Block())

        def wide(a):
            return a.unsqueeze(2).broadcast_to([P, NT, E])

        @block.vector
        def _(dve):
            count = [0]

            def then(ins):
                count[0] += 1
                ins.then_inc(step, 1)
                dve.wait_ge(step, count[0])

            lg = logits[:, :, 0:E]
            then(dve.tensor_reduce(top[:, 0, :], lg, AX.X, ALU.max))
            dve.tensor_tensor(ex[:], lg, wide(top[:, 0, :]), ALU.subtract).then_inc(shifted, 1)
            dve.wait_ge(exped, 2)
            then(dve.tensor_reduce(top[:, 1, :], ex[:], AX.X, ALU.add))
            then(dve.reciprocal(top[:, 2, :], top[:, 1, :]))
            then(dve.tensor_tensor(prob[:], ex[:], wide(top[:, 2, :]), ALU.mult))
            then(dve.tensor_reduce(top[:, 0, :], prob[:], AX.X, ALU.max))
            then(dve.tensor_tensor(key[:], prob[:], wide(top[:, 0, :]), ALU.is_equal))
            then(dve.tensor_tensor(key[:], key[:], rank[:].unsqueeze(1).broadcast_to([P, NT, E]), ALU.mult))
            then(dve.tensor_reduce(top[:, 3, :], key[:], AX.X, ALU.max))
            then(dve.tensor_tensor(first[:], key[:], wide(top[:, 3, :]), ALU.is_equal))
            then(dve.scalar_tensor_tensor(rest[:], first[:], -2.0, prob[:], ALU.mult, ALU.add))
            then(dve.tensor_reduce(top[:, 1, :], rest[:], AX.X, ALU.max))
            then(dve.tensor_tensor(key[:], rest[:], wide(top[:, 1, :]), ALU.is_equal))
            then(dve.tensor_tensor(key[:], key[:], rank[:].unsqueeze(1).broadcast_to([P, NT, E]), ALU.mult))
            then(dve.tensor_reduce(top[:, 3, :], key[:], AX.X, ALU.max))
            then(dve.tensor_tensor(both[:], key[:], wide(top[:, 3, :]), ALU.is_equal))
            then(dve.tensor_tensor(both[:], both[:], first[:], ALU.add))
            then(dve.tensor_tensor(top[:, 4, :], top[:, 0, :], top[:, 1, :], ALU.add))
            then(dve.reciprocal(top[:, 5, :], top[:, 4, :]))
            then(dve.tensor_tensor(both[:], both[:], prob[:], ALU.mult))
            then(dve.tensor_tensor(comb[:, :, 0:E], both[:], wide(top[:, 5, :]), ALU.mult))
            then(dve.tensor_scalar(ex9[:], ex9[:], 1.0, None, ALU.add))
            then(dve.reciprocal(comb[:, :, E:NE], ex9[:]))
            then(dve.tensor_copy(parts[:, :, 0, :], comb[:]))
            then(dve.tensor_tensor(resid[:], comb[:], parts[:, :, 0, :], ALU.subtract))
            then(dve.tensor_copy(parts[:, :, 1, :], resid[:]))
            dve.tensor_tensor(parts[:, :, 2, :], resid[:], parts[:, :, 1, :], ALU.subtract).then_inc(split, 1)

        @block.scalar
        def _(act):
            act.activation(ex9[:], logits[:, :, E:NE], ACT.Exp, scale=-1.0).then_inc(exped, 1)
            act.wait_ge(shifted, 1)
            act.activation(ex[:], ex[:], ACT.Exp).then_inc(exped, 1)
            for b in range(NB):
                act.wait_ge(turned, b + 1)
                act.activation(combT[:, b * BLK:(b + 1) * BLK],
                               ps[0:3 * NE, b % 2, :].bitcast(BF16)[:, 0:BLK], ACT.Copy).then_inc(kept, 1)

        @block.tensor
        def _(pe):
            pe.wait_ge(split, 1)
            for b in range(NB):
                if b >= 2:
                    pe.wait_ge(kept, b - 1)
                for j in range(TPB):
                    last = pe.transpose(ps[0:3 * NE, b % 2, :].bitcast(BF16)[:, j * P:(j + 1) * P],
                                        parts[:, b * TPB + j, :, :].rearrange("p a e -> p (a e)"), identb[:])
                last.then_inc(turned, 1)


def expert_phase(nc, sem, tag, ps, x, xnT, wgate, wup, wdown, expert_rows, combT, ident, work, out_dram,
                 head_buffers=None):
    gated = sem(tag + "_gated")
    upped = sem(tag + "_upped")
    spread = sem(tag + "_spread")
    silued = sem(tag + "_silued")
    product = sem(tag + "_product")
    hidden_ready = sem(tag + "_hidden")
    summed = sem(tag + "_summed")
    summed_kept = sem(tag + "_summed_kept")
    turned = sem(tag + "_turned")
    added = sem(tag + "_added")
    stored = sem(tag + "_stored")
    zeroed = sem(tag + "_zeroed")
    hidden = work[:, 0:CH * BLK].rearrange("p (c t) -> p c t", c=CH)
    rows = [min(P, R - c * P) for c in range(CH)]
    with ExitStack() as tmp:
        silu = tmp.enter_context(nc.sbuf_tensor(tag + "_silu", [P, 2, BLK], F32))
        prod = tmp.enter_context(nc.sbuf_tensor(tag + "_prod", [P, 2, BLK], F32))
        yT = tmp.enter_context(nc.sbuf_tensor(tag + "_yT", [P, BLK], F32))
        block = tmp.enter_context(nc.Block())
        GATE, UP, SPREAD, Y, YT = 0, 2, 4, 6, 7

        @block.tensor
        def _(pe):
            with pe.Fori(0, NB // 2) as it:
                for par in range(2):
                    blk = it * 2 + par
                    tokens = bass.ds(blk * BLK, BLK)

                    def up(c):
                        i, cols = (par + c) % 2, slice(c * P, (c + 1) * P)
                        pe.matmul(ps[:, GATE + i, :], wgate[:, cols], xnT[:, tokens],
                                  start=True, stop=True).then_inc(gated, 1)
                        pe.matmul(ps[:, UP + i, :], wup[:, cols], xnT[:, tokens],
                                  start=True, stop=True).then_inc(upped, 1)
                        pe.matmul(ps[:, SPREAD + i, :], expert_rows[:, cols], combT[:, tokens],
                                  start=True, stop=True).then_inc(spread, 1)

                    def down(c):
                        return pe.matmul(ps[:, Y, :], wdown[0:rows[c], c, :], hidden[0:rows[c], c, :],
                                         start=(c == 0), stop=(c == CH - 1))

                    up(0)
                    up(1)
                    for c in range(2, CH):
                        pe.wait_ge(hidden_ready, blk * CH + c - 1)
                        up(c)
                        if c == 2:
                            pe.wait_ge(summed_kept, blk + PRIME)
                        down(c - 2)
                    pe.wait_ge(hidden_ready, blk * CH + CH - 1)
                    down(CH - 2)
                    pe.wait_ge(hidden_ready, blk * CH + CH)
                    down(CH - 1).then_inc(summed, 1)
                    pe.wait_ge(summed_kept, blk + 1 + PRIME)
                    pe.wait_ge(added, blk + PRIME)
                    for j in range(TPB):
                        last = pe.transpose(ps[:, YT, j * P:(j + 1) * P], yT[:, j * P:(j + 1) * P], ident[:])
                    last.then_inc(turned, 1)

        @block.scalar
        def _(act):
            prime(act, summed_kept)
            with act.Fori(0, NB // 2) as it:
                for par in range(2):
                    blk = it * 2 + par
                    for c in range(CH):
                        i = (par + c) % 2
                        act.wait_ge(gated, blk * CH + c + 1)
                        act.activation(silu[:, i, :], ps[:, GATE + i, :], ACT.Silu).then_inc(silued, 1)
                    act.wait_ge(summed, blk + 1)
                    act.activation(yT[:], ps[:, Y, :], ACT.Copy).then_inc(summed_kept, 1)

        @block.vector
        def _(dve):
            prime(dve, added)
            with dve.Fori(0, NB // 2) as it:
                for par in range(2):
                    blk = it * 2 + par
                    for c in range(CH):
                        i = (par + c) % 2
                        dve.wait_ge(silued, blk * CH + c + 1)
                        dve.wait_ge(upped, blk * CH + c + 1)
                        dve.tensor_tensor(prod[:, i, :], silu[:, i, :], ps[:, UP + i, :],
                                          ALU.mult).then_inc(product, 1)
                        dve.wait_ge(product, blk * CH + c + 1)
                        dve.wait_ge(spread, blk * CH + c + 1)
                        dve.tensor_tensor(hidden[:, c, :], prod[:, i, :], ps[:, SPREAD + i, :],
                                          ALU.mult).then_inc(hidden_ready, 1)
                    dve.wait_ge(turned, blk + 1)
                    tiles = x[:, bass.ds(blk * TPB, TPB), :].rearrange("p n d -> p (n d)")
                    dve.scalar_tensor_tensor(tiles, ps[:, YT, :], 0.5, tiles, ALU.mult, ALU.add).then_inc(added, 1)

        if head_buffers is not None:
            @block.gpsimd
            def _(pool):
                q_head, k_head, vals = head_buffers
                for i in range(BUFS):
                    pool.memset(q_head[i][:], 0.0)
                    pool.memset(k_head[i][:], 1.0)
                    pool.memset(vals[i][:, :, HD:32], 0.0).then_inc(zeroed, 1)
                pool.wait_ge(zeroed, BUFS)
                for i in range(BUFS):
                    pool.memset(vals[i][:, :, HD:HD1], 1.0)

        if out_dram is not None:
            @block.sync
            def _(sp):
                with sp.Fori(0, NB) as blk:
                    sp.wait_ge(added, blk + 1 + PRIME)
                    sp.dma_start(out_dram[:, bass.ds(blk * TPB, TPB), :],
                                 x[:, bass.ds(blk * TPB, TPB), :]).then_inc(stored, 16)
                sp.wait_ge(stored, 16 * NB)


def qkv_phase(nc, sem, ps, xnT, weights, norm_w, head_mean, swap, rope, ident, v, q_rows, k_rows):
    projected = sem("qk_projected")
    squared = sem("qk_squared")
    meaned = sem("qk_meaned")
    eps_set = sem("qk_eps_set")
    rooted = sem("qk_rooted")
    raised = sem("qk_raised")
    normed = sem("qk_normed")
    swapped = sem("qk_swapped")
    turning = sem("qk_turning")
    split = sem("qk_split")
    part0 = sem("qk_part0")
    part1 = sem("qk_part1")
    part2 = sem("qk_part2")
    v_kept = sem("qk_v_kept")
    v_turned = sem("qk_v_turned")
    v_done = sem("qk_v_done")
    stored = sem("qk_stored")
    SLOTS = {j: [n for n, pair in enumerate(PAIRS) if pair[0] == j] for j in range(3)}
    KSLOTS = {j: [n for n, pair in enumerate(PAIRS) if pair[1] == j] for j in range(3)}
    with ExitStack() as tmp:
        def tb(name, shape, dt=F32):
            return tmp.enter_context(nc.sbuf_tensor("qk_" + name, shape, dt))
        sq = tb("sq", [P, 2, BLK])
        eps = tb("eps", [P, 1])
        root = tb("root", [P, 2, BLK])
        rstd = tb("rstd", [P, 2, BLK])
        qn = tb("qn", [P, 2, BLK])
        rot = tb("rot", [P, 2, BLK])
        r1 = tb("r1", [P, 2, BLK])
        parts = tb("parts", [P, 2, 3, BLK], BF16)
        vT = tb("vT", [P, BLK])
        block = tmp.enter_context(nc.Block())
        N_ROPE = 2 * 3

        @block.tensor
        def _(pe):
            prime(pe, meaned, v_turned)
            with pe.Fori(0, BATCH) as b:
                for n in range(BPS):
                    blk = b * BPS + n
                    pe.wait_ge(part0, blk * 2 + PRIME)
                    pe.wait_ge(v_kept, blk + PRIME)
                    for i in range(3):
                        pe.matmul(ps[:, i, :], weights[i][:], xnT[:, bass.ds(blk * BLK, BLK)],
                                  start=True, stop=True).then_inc(projected, 1)
                    for i in range(2):
                        pe.wait_ge(squared, blk * 2 + i + 1)
                        pe.matmul(ps[:, 3 + i, :], head_mean[:], sq[:, i, :], start=True, stop=True).then_inc(meaned, 1)
                    pe.wait_ge(v_kept, blk + 1 + PRIME)
                    pe.wait_ge(v_done, blk + PRIME)
                    for j in range(TPB):
                        last = pe.transpose(ps[:, 5, j * P:(j + 1) * P], vT[:, j * P:(j + 1) * P], ident[:])
                    last.then_inc(v_turned, 1)
                    if n == BPS - 1:
                        for i in range(2):
                            pe.wait_ge(normed, blk * 2 + i + 1)
                            pe.matmul(ps[:, 6 + i, :], swap[:], qn[:, i, :], start=True, stop=True).then_inc(swapped, 1)

        @block.scalar
        def _(act):
            prime(act, v_kept, v_done)
            act.wait_ge(eps_set, 1)
            with act.Fori(0, BATCH) as b:
                for n in range(BPS):
                    blk = b * BPS + n
                    for i in range(2):
                        act.wait_ge(projected, blk * 3 + i + 1)
                        act.wait_ge(meaned, blk * 2 + PRIME)
                        act.activation(sq[:, i, :], ps[:, i, :], ACT.Square).then_inc(squared, 1)
                    for i in range(2):
                        act.wait_ge(meaned, blk * 2 + i + 1 + PRIME)
                        act.wait_ge(raised, blk * 2 + PRIME)
                        act.activation(root[:, i, :], ps[:, 3 + i, :], ACT.Sqrt, bias=eps[:]).then_inc(rooted, 1)
                    act.wait_ge(projected, blk * 3 + 3)
                    act.wait_ge(v_turned, blk + PRIME)
                    act.activation(vT[:], ps[:, 2, :], ACT.Copy).then_inc(v_kept, 1)
                    act.wait_ge(v_turned, blk + 1 + PRIME)
                    act.activation(
                        v[:, b, :, n * TPB:(n + 1) * TPB, :].rearrange("p h t d -> p t h d"),
                        ps[:, 5, :].rearrange("p (t h d) -> p t h d", t=TPB, h=HEADS), ACT.Copy).then_inc(v_done, 1)

        @block.vector
        def _(dve):
            prime(dve, raised, part0)
            dve.memset(eps[:], RMS_EPS).then_inc(eps_set, 1)
            with dve.Fori(0, BATCH) as b:
                for n in range(BPS):
                    blk = b * BPS + n
                    for i in range(2):
                        dve.wait_ge(rooted, blk * 2 + i + 1)
                        dve.reciprocal(rstd[:, i, :], root[:, i, :]).then_inc(raised, 1)
                    for i in range(2):
                        dve.wait_ge(raised, blk * 2 + i + 1 + PRIME)
                        dve.scalar_tensor_tensor(qn[:, i, :], ps[:, i, :], norm_w[:, i:i + 1], rstd[:, i, :],
                                                 ALU.mult, ALU.mult).then_inc(normed, 1)
                    for i in range(2):
                        turned = qn[:, i, :]
                        dve.wait_ge(normed, blk * 2 + i + 1)
                        if n == BPS - 1:
                            at = b * N_ROPE + 3 * i
                            dve.wait_ge(swapped, b * 2 + i + 1)
                            dve.tensor_tensor(rot[:, i, :], qn[:, i, :], rope[:, 0, :], ALU.mult).then_inc(turning, 1)
                            dve.tensor_tensor(r1[:, i, :], ps[:, 6 + i, :], rope[:, 1, :], ALU.mult).then_inc(turning, 1)
                            dve.wait_ge(turning, at + 2)
                            dve.tensor_tensor(rot[:, i, :], rot[:, i, :], r1[:, i, :], ALU.add).then_inc(turning, 1)
                            dve.wait_ge(turning, at + 3)
                            turned = rot[:, i, :]
                        dve.wait_ge(stored, blk * (2 * len(PAIRS)) * 16 + PRIME)
                        dve.tensor_copy(parts[:, i, 0, :], turned).then_inc(part0, 1)
                        dve.wait_ge(part0, blk * 2 + i + 1 + PRIME)
                        dve.tensor_tensor(r1[:, i, :], turned, parts[:, i, 0, :], ALU.subtract).then_inc(split, 1)
                        dve.wait_ge(split, blk * 4 + 2 * i + 1)
                        dve.tensor_copy(parts[:, i, 1, :], r1[:, i, :]).then_inc(part1, 1)
                        dve.wait_ge(part1, blk * 2 + i + 1)
                        dve.tensor_tensor(parts[:, i, 2, :], r1[:, i, :], parts[:, i, 1, :],
                                          ALU.subtract).then_inc(split, 1)

        @block.sync
        def _(sp):
            prime(sp, stored)
            with sp.Fori(0, BATCH) as b:
                for n in range(BPS):
                    blk = b * BPS + n
                    for i, (rows, slots) in enumerate(((q_rows, SLOTS), (k_rows, KSLOTS))):
                        heads = rows[bass.ds(b * HEADS, HEADS), :, n * BLK:(n + 1) * BLK]
                        for j in range(3):
                            if j < 2:
                                sp.wait_ge((part0, part1)[j], blk * 2 + i + 1 + (PRIME if j == 0 else 0))
                            else:
                                sp.wait_ge(split, blk * 4 + 2 * i + 2)
                            for slot in slots[j]:
                                sp.dma_start(heads[:, slot * HD:(slot + 1) * HD, :], parts[:, i, j, :]).then_inc(stored, 16)
            sp.wait_ge(stored, 16 * 2 * len(PAIRS) * NB + PRIME)


def attention_phase(nc, sem, ps, v, identb, work, q, k, vals, q_rows, k_rows, o_rows, den_rows):
    CHUNKS = SEQ // BLK
    STEPS = KT * CHUNKS
    AHEAD, LAG = 2, 11
    TURNS = BH - AHEAD
    assert TURNS % BUFS == 0 and STEPS % BUFS == 1
    qk_loaded = [sem(f"at_qk_loaded{i}") for i in range(BUFS)]
    max_scored = sem("at_max_scored")
    max_reduced = sem("at_max_reduced")
    max_step = sem("at_max_step")
    max_turned = sem("at_max_turned")
    max_kept = sem("at_max_kept")
    max_placed = sem("at_max_placed")
    scored = sem("at_scored")
    exped = sem("at_exped")
    weighed = sem("at_weighed")
    values_placed = sem("at_values_placed")
    sums_kept = sem("at_sums_kept")
    sums_stored = sem("at_sums_stored")
    SUM_DMAS = 2 * CHUNKS
    VSTEPS = 5
    prob = work[:, 0:PROBS * CHUNKS * BLK].rearrange("p (g c t) -> p g c t", g=PROBS, c=CHUNKS)
    with ExitStack() as tmp:
        def tb(name, shape, dt=F32):
            return tmp.enter_context(nc.sbuf_tensor("at_" + name, shape, dt))
        mx = tb("mx", [P, KT, CHUNKS])
        neg = tb("neg", [P, KT])
        res = tb("res", [P, KT])
        mparts = tb("mparts", [P, MR, KT], BF16)
        mrows = tb("mrows", [MR * KT, P], BF16)
        sums = tb("sums", [P, BLK])
        block = tmp.enter_context(nc.Block())
        S, M, O, X = 0, 3, 6, 7

        @block.gpsimd
        def _(pool):
            def place(h, i):
                head = v[:].rearrange("p b h t d -> p (b h) t d")[:, h, :, :]
                pool.tensor_copy(vals[i][:, :, 0:HD], head).then_inc(values_placed, 1)

            for i in range(BUFS):
                place(i, i)

            def replace(h, i):
                pool.wait_ge(weighed, (h + 1) * KT + PRIME)
                place(h + BUFS, i)

            with pool.Fori(0, BH // BUFS - 1) as it:
                for i in range(BUFS):
                    replace(it * BUFS + i, i)
            for h in range((BH // BUFS - 1) * BUFS, BH - BUFS):
                replace(h, h % BUFS)

        @block.sync
        def _(sp):
            def load(h, i):
                sp.dma_start(q[i][0:KR, :], q_rows[h]).then_inc(qk_loaded[i], 16)
                sp.dma_start(k[i][0:KR, :], k_rows[h]).then_inc(qk_loaded[i], 16)

            def place_maxima(h, i):
                sp.wait_ge(max_kept, h + 1)
                sp.dma_start(q[i][MROW:MROW + MR, :], mrows[:]).then_inc(max_placed, 16)

            def store_sums(h):
                sp.wait_ge(sums_kept, h + 1 + PRIME)
                for c in range(CHUNKS):
                    cols = slice(c * BLK, (c + 1) * BLK)
                    sp.dma_start(o_rows[h][:, cols], sums[32 * c:32 * c + HD, :]).then_inc(sums_stored, 16)
                    sp.dma_start(den_rows[h][:, cols], sums[32 * c + HD:32 * c + HD1, :]).then_inc(sums_stored, 16)

            def turn(h, i):
                place_maxima(h + 1, (i + 1) % BUFS)
                sp.wait_ge(weighed, (h + 1) * KT + PRIME)
                load(h + BUFS, i)
                store_sums(h)

            prime(sp, sums_stored)
            for h in range(BUFS):
                load(h, h)
            place_maxima(0, 0)
            with sp.Fori(0, BH // BUFS - 1) as it:
                for i in range(BUFS):
                    turn(it * BUFS + i, i)
            for h in range((BH // BUFS - 1) * BUFS, BH):
                if h < BH - BUFS:
                    turn(h, h % BUFS)
                else:
                    if h < BH - 1:
                        place_maxima(h + 1, (h + 1) % BUFS)
                    store_sums(h)
            sp.wait_ge(sums_stored, 16 * SUM_DMAS * BH + PRIME)

        @block.scalar
        def _(act):
            def exps(h, i, g):
                for c in range(CHUNKS):
                    n = h * STEPS + g * CHUNKS + c
                    act.wait_ge(scored, n + 1)
                    act.activation(prob[:, g % PROBS, c, :], ps[:, S + (i + g * CHUNKS + c) % BUFS, :],
                                   ACT.Exp).then_inc(exped, 1)

            def keep_sums(h):
                act.wait_ge(weighed, (h + 1) * KT + PRIME)
                act.wait_ge(sums_stored, 16 * SUM_DMAS * h + PRIME)
                act.activation(sums[:], ps[:, O, :], ACT.Copy).then_inc(sums_kept, 1)

            def keep_maxima(h):
                act.wait_ge(max_turned, h + 1 + PRIME)
                if not (isinstance(h, int) and h == 0):
                    act.wait_ge(max_placed, 16 * h)
                act.activation(mrows[:], ps[0:MR * KT, X, 0:P], ACT.Copy).then_inc(max_kept, 1)

            def turn(h, i, last=False):
                for g in range(1, KT):
                    if not (isinstance(h, int) and h == 0 and g < PROBS):
                        act.wait_ge(weighed, h * KT + max(g - PROBS, -1) + 1 + PRIME)
                    exps(h, i, g)
                    if g == LAG + 2 and not last:
                        keep_maxima(h + 1)
                if not last:
                    act.wait_ge(weighed, (h + 1) * KT - PROBS + 1 + PRIME)
                    exps(h + 1, i + 1, 0)
                keep_sums(h)

            prime(act, sums_kept)
            keep_maxima(0)
            exps(0, 0, 0)
            with act.Fori(0, TURNS // BUFS) as it:
                for i in range(BUFS):
                    turn(it * BUFS + i, i)
            turn(BH - 2, (BH - 2) % BUFS)
            turn(BH - 1, (BH - 1) % BUFS, last=True)

        @block.tensor
        def _(pe):
            def maxima(h, i, j):
                n, c = h * STEPS + j, j % CHUNKS
                if not (isinstance(n, int) and n < BUFS):
                    pe.wait_ge(max_reduced, n - BUFS + 1)
                pe.matmul(ps[:, M + (i + j) % BUFS, :], q[i][0:MROW, (j // CHUNKS) * P:(j // CHUNKS + 1) * P],
                          k[i][0:MROW, c * BLK:(c + 1) * BLK], start=True, stop=True).then_inc(max_scored, 1)

            def turn_maxima(h):
                pe.wait_ge(max_step, (h + 1) * VSTEPS)
                pe.matmul(ps[0:MR * KT, X, 0:P], mparts[:].rearrange("p a t -> p (a t)"), identb[:],
                          start=True, stop=True).then_inc(max_turned, 1)

            def scores(h, i, g, c):
                n = h * STEPS + g * CHUNKS + c
                if not (isinstance(n, int) and n < BUFS):
                    pe.wait_ge(exped, n - BUFS + 1)
                pe.matmul(ps[:, S + (i + g * CHUNKS + c) % BUFS, :], k[i][:, g * P:(g + 1) * P],
                          q[i][:, c * BLK:(c + 1) * BLK], start=True, stop=True).then_inc(scored, 1)

            def weigh(h, i, g):
                pe.wait_ge(exped, h * STEPS + (g + 1) * CHUNKS)
                if g == 0:
                    pe.wait_ge(values_placed, h + 1)
                    pe.wait_ge(sums_kept, h + PRIME)
                for c in range(CHUNKS):
                    last = pe.matmul(ps[32 * c:32 * c + 32, O, :], vals[i][:, g, :], prob[:, g % PROBS, c, :],
                                     start=(g == 0), stop=(g == KT - 1), skip_group_check=True)
                last.then_inc(weighed, 1)

            def turn(h, i, loads=None, last=False):
                nxt, far = (i + 1) % BUFS, (i + AHEAD) % BUFS
                for g in range(1, KT + 1):
                    if g == LAG + 1 and loads is not None:
                        pe.wait_ge(qk_loaded[far], 16 * 2 * loads)
                    if g == KT and not last:
                        pe.wait_ge(max_placed, 16 * (h + 2))
                    for c in range(CHUNKS):
                        if g < KT:
                            scores(h, i, g, c)
                        elif not last:
                            scores(h + 1, nxt, 0, c)
                        if g <= LAG and not last:
                            maxima(h + 1, nxt, (KT - LAG + g - 1) * CHUNKS + c)
                        elif g > LAG and loads is not None:
                            maxima(h + AHEAD, far, (g - LAG - 1) * CHUNKS + c)
                    weigh(h, i, g - 1)
                    if g == LAG + 1 and not last:
                        turn_maxima(h + 1)

            prime(pe, weighed, max_turned)
            for h in range(AHEAD):
                pe.wait_ge(qk_loaded[h], 16 * 2)
                for j in range(STEPS if h == 0 else (KT - LAG) * CHUNKS):
                    maxima(h, h, j)
                if h == 0:
                    turn_maxima(0)
            pe.wait_ge(max_placed, 16)
            for c in range(CHUNKS):
                scores(0, 0, 0, c)
            with pe.Fori(0, TURNS // BUFS) as it:
                for i in range(BUFS):
                    turn(it * BUFS + i, i, loads=it + 1 + (i + AHEAD) // BUFS)
            turn(BH - 2, (BH - 2) % BUFS)
            turn(BH - 1, (BH - 1) % BUFS, last=True)

        @block.vector
        def _(dve):
            def maxima(h, i):
                for j in range(STEPS):
                    dve.wait_ge(max_scored, h * STEPS + j + 1)
                    dve.tensor_reduce(mx[:, j // CHUNKS, j % CHUNKS:j % CHUNKS + 1], ps[:, M + (i + j) % BUFS, :],
                                      AX.X, ALU.max).then_inc(max_reduced, 1)
                at = h * VSTEPS
                dve.wait_ge(max_reduced, h * STEPS + STEPS)
                dve.tensor_reduce(neg[:], mx[:], AX.X, ALU.max, negate=True).then_inc(max_step, 1)
                dve.wait_ge(max_step, at + 1)
                dve.wait_ge(max_turned, h + PRIME)
                dve.tensor_copy(mparts[:, 0, :], neg[:]).then_inc(max_step, 1)
                dve.wait_ge(max_step, at + 2)
                dve.tensor_tensor(res[:], neg[:], mparts[:, 0, :], ALU.subtract).then_inc(max_step, 1)
                dve.wait_ge(max_step, at + 3)
                dve.tensor_copy(mparts[:, 1, :], res[:]).then_inc(max_step, 1)
                dve.wait_ge(max_step, at + 4)
                dve.tensor_tensor(mparts[:, 2, :], res[:], mparts[:, 1, :], ALU.subtract).then_inc(max_step, 1)

            with dve.Fori(0, TURNS // BUFS) as it:
                for i in range(BUFS):
                    maxima(it * BUFS + i, i)
            for h in range(TURNS, BH):
                maxima(h, h % BUFS)


def output_phase(nc, sem, ps, x, woT, head_rows, o_rows, den_rows):
    loaded = [sem(f"op_loaded{i}") for i in range(2)]
    inverted = sem("op_inverted")
    spread = sem("op_spread")
    divided = sem("op_divided")
    projected = sem("op_projected")
    added = sem("op_added")
    with ExitStack() as tmp:
        def tb(name, shape):
            return tmp.enter_context(nc.sbuf_tensor("op_" + name, shape, F32))
        o = tb("o", [P, 2, BLK])
        den = tb("den", [HEADS, 2, BLK])
        inv = tb("inv", [HEADS, 2, BLK])
        oT = tb("oT", [P, 2, BLK])
        block = tmp.enter_context(nc.Block())

        @block.sync
        def _(sp):
            with sp.Fori(0, BATCH) as b:
                for n in range(BPS):
                    blk, i = b * BPS + n, n % 2
                    if n >= 2:
                        sp.wait_ge(divided, blk - 1 + PRIME)
                    else:
                        sp.wait_ge(divided, b * BPS + PRIME)
                    cols = slice(n * BLK, (n + 1) * BLK)
                    heads = bass.ds(b * HEADS, HEADS)
                    sp.dma_start(o[:, i, :], o_rows[heads, :, cols]).then_inc(loaded[i], 16)
                    sp.dma_start(den[:, i, :], den_rows[heads, :, cols]).then_inc(loaded[i], 16)

        @block.vector
        def _(dve):
            prime(dve, divided)
            with dve.Fori(0, BATCH) as b:
                for n in range(BPS):
                    blk, i = b * BPS + n, n % 2
                    dve.wait_ge(loaded[i], (b * (BPS // 2) + n // 2 + 1) * 32)
                    dve.reciprocal(inv[:, i, :], den[:, i, :]).then_inc(inverted, 1)
                    dve.wait_ge(spread, blk + 1)
                    dve.tensor_tensor(oT[:, i, :], o[:, i, :], ps[:, i, :], ALU.mult).then_inc(divided, 1)
                    dve.wait_ge(projected, blk + 1)
                    tiles = x[:, bass.ds(blk * TPB, TPB), :].rearrange("p n d -> p (n d)")
                    dve.tensor_tensor(tiles, ps[:, 2 + i, :], tiles, ALU.add).then_inc(added, 1)

        @block.tensor
        def _(pe):
            with pe.Fori(0, BATCH) as b:
                for n in range(BPS):
                    blk, i = b * BPS + n, n % 2
                    pe.wait_ge(inverted, blk + 1)
                    pe.matmul(ps[:, i, :], head_rows[:], inv[:, i, :], start=True, stop=True).then_inc(spread, 1)
                    pe.wait_ge(divided, blk + 1 + PRIME)
                    for j in range(TPB):
                        last = pe.matmul(ps[:, 2 + i, j * D:(j + 1) * D], oT[:, i, j * P:(j + 1) * P], woT[:],
                                         start=True, stop=True)
                    last.then_inc(projected, 1)


_INS = ["L0_attn_x", "L0_attn_rope_cos", "L0_attn_rope_sin", "L0_attn_wq", "L0_attn_wk", "L0_attn_wv",
        "L0_attn_wo", "L0_attn_q_norm_w", "L0_attn_k_norm_w", "L0_ffn_gate_w", "L0_ffn_w_gate",
        "L0_ffn_w_up", "L0_ffn_w_down", "L0_ffn_sw_gate", "L0_ffn_sw_up", "L0_ffn_sw_down",
        "L0_ffn_shared_gate_w"]


def _constants():
    import numpy as np

    row = np.arange(P)
    col = np.arange(CH * P)
    expert = np.tile(np.arange(E + 1), 3)
    return {
        "ident": np.eye(P, dtype=np.float32),
        "expert_rows": (expert[:, None] == col[None, :] // I).astype(np.float32),
        "head_rows": (np.arange(HEADS)[:, None] == row[None, :] // HD).astype(np.float32),
        "dim_rows": (np.arange(HD)[:, None] == row[None, :] % HD).astype(np.float32),
        "pair_rows": np.stack([
            (np.arange(HD // 2)[:, None] == row[None, :] % HD // 2).astype(np.float32),
            (np.arange(HD // 2)[:, None] == row[None, :] % HD // 2) * np.where(row % 2 == 0, -1, 1).astype(np.float32),
        ], axis=1).astype(np.float32),
        "head_mean": (row[:, None] // HD == row[None, :] // HD).astype(np.float32) / HD,
        "swap": (row[:, None] == (row[None, :] ^ 1)).astype(np.float32),
        "rank": np.tile(np.arange(E, 0, -1, dtype=np.float32), (P, 1)),
    }


def kernel(**inputs):
    import numpy as _np
    import concourse.bacc as _bacc
    from concourse import mybir as _mybir
    from concourse.bass_utils import run_bass_kernel_spmd as _run

    nc = _bacc.Bacc("TRN2", target_bir_lowering=False, num_devices=1)
    arrays, args = {}, []
    for name in _INS:
        a = _np.ascontiguousarray(inputs[name])
        arrays[f"in_{name}_dram"] = a
        args.append(nc.dram_tensor(f"in_{name}_dram", a.shape, _mybir.dt.from_np(a.dtype), kind="ExternalInput").ap())
    for name, a in _constants().items():
        arrays[f"const_{name}_dram"] = a
        args.append(nc.dram_tensor(f"const_{name}_dram", a.shape, _mybir.dt.from_np(a.dtype), kind="ExternalInput").ap())
    args.append(nc.dram_tensor("out_0_dram", (BATCH, SEQ, D), F32, kind="ExternalOutput").ap())
    build(nc, *args)
    r = _run(nc, [arrays], core_ids=[0])
    return r.results[0]["out_0_dram"]
```

```python
from contextlib import ExitStack

import concourse.bass as bass
from concourse import mybir

F32 = mybir.dt.float32
F32R = mybir.dt.float32r
BF16 = mybir.dt.bfloat16
ALU = mybir.AluOpType
ACT = mybir.ActivationFunctionType
AX = mybir.AxisListType

P = 128
D = 128
BATCH, SEQ = 2, 2048
T = BATCH * SEQ
NT = T // P
BLK = 512
NB = T // BLK
TPB = BLK // P
BPS = SEQ // BLK
E = 8
I = 176
R = (E + 1) * I
CH = -(-R // P)
HEADS, HD = 16, 8
HD1 = HD + 1
BH = BATCH * HEADS
PATCH = 508
KT = SEQ // P
LN_EPS, RMS_EPS = 1e-5, 1e-6
BUFS = 3
PROBS = 4
PRIME = 1

PAIRS = [(0, 0), (0, 1), (0, 2), (1, 0), (1, 1), (2, 0)]
KR = len(PAIRS) * HD
MR = 3
MROW = 96


HI, LO = 0, 1
PASSES = [(HI, HI), (HI, LO), (LO, HI)]


def prime(eng, *sems):
    for s in sems:
        eng.sem_inc(s, PRIME)


def build(nc, x_in, rope_cos, rope_sin, wq, wk, wv, wo, q_norm_w, k_norm_w, gate_w, w_gate, w_up,
          w_down, sw_gate, sw_up, sw_down, shared_gate_w, c_ident, c_expert_rows, c_block_rows,
          c_dim_rows, c_pair_rows, c_head_mean, c_swap, c_rank, out):
    x_dram = x_in.rearrange("b (n p) d -> p (b n) d", p=P)
    out_dram = out.rearrange("b (n p) d -> p (b n) d", p=P)
    q_rows = nc.dram_tensor("q_rows", (BH, HD, 3, SEQ), BF16).ap()
    k_rows = nc.dram_tensor("k_rows", (BH, HD, 3, SEQ), BF16).ap()
    o_rows = nc.dram_tensor("o_rows", (BH, HD, SEQ), F32).ap()
    den_rows = nc.dram_tensor("den_rows", (BH, 1, SEQ), F32).ap()

    nc.disable_value_cache = True
    with ExitStack() as ctx:
        def sb(name, shape, dt=F32):
            return ctx.enter_context(nc.sbuf_tensor(name, shape, dt))

        def sem(name):
            return ctx.enter_context(nc.semaphore(name))

        ps = ctx.enter_context(nc.psum_tensor("ps", [P, 8, BLK], F32))

        x = sb("x", [P, NT, D])
        stats = sb("stats", [P, NT, 6])
        xnT = [sb("xnT" + part, [P, T], F32R) for part in ("_hi", "_lo")]
        wgate = [sb("wgate" + part, [P, CH * P], F32R) for part in ("_hi", "_lo")]
        wup = [sb("wup" + part, [P, CH * P], F32R) for part in ("_hi", "_lo")]
        wdown = [sb("wdown" + part, [P, CH, D], F32R) for part in ("_hi", "_lo")]
        ident = sb("ident", [P, P])
        identb = sb("identb", [P, P], BF16)
        expert_rows = sb("expert_rows", [3 * (E + 1), CH * P], BF16)
        block_rows = sb("block_rows", [P, NB, P])
        head_mean = sb("head_mean", [P, HEADS])
        swap = sb("swap", [P, P])
        rank = sb("rank", [P, E])
        gateT = [sb("gateT" + part, [P, P], F32R) for part in ("_hi", "_lo")]
        wqT = [sb("wqT" + part, [P, D], F32R) for part in ("_hi", "_lo")]
        wkT = [sb("wkT" + part, [P, D], F32R) for part in ("_hi", "_lo")]
        wvT = [sb("wvT" + part, [P, D], F32R) for part in ("_hi", "_lo")]
        woT = sb("woT", [P, D])
        norm_w = sb("norm_w", [P, 2])
        rope = sb("rope", [P, 2, BLK])
        logits = sb("logits", [P, NT, E + 1])
        combT = sb("combT", [3 * (E + 1), T], BF16)
        v = sb("v", [P, BATCH, HEADS, KT, HD])
        q_head = [sb(f"q_head{i}", [P, SEQ], BF16) for i in range(BUFS)]
        k_head = [sb(f"k_head{i}", [P, SEQ], BF16) for i in range(BUFS)]
        vals = [sb(f"vals{i}", [P, KT, 32]) for i in range(BUFS)]

        with ExitStack() as weights_ctx:
            raw_w = [weights_ctx.enter_context(nc.sbuf_tensor("raw_" + w, [P, CH * P], F32))
                     for w in ("wgate", "wup", "wdown")]
            load_phase(nc, sem, sb, locals())
            norm_phase(nc, sem, "n1", ps, x, stats, xnT, ident, gateT, logits,
                       split=list(zip(raw_w, (wgate, wup, wdown))))
        routing_phase(nc, sem, "r1", ps, logits, rank, identb, combT)
        expert_phase(nc, sem, "e1", ps, x, xnT, wgate, wup, wdown, expert_rows, combT, ident,
                     stats=stats)
        norm_phase(nc, sem, "n2", ps, x, stats, xnT, ident)
        qkv_phase(nc, sem, ps, xnT, (wqT, wkT, wvT), norm_w, head_mean, block_rows, swap, rope,
                  ident, v, q_rows, k_rows)
        attention_phase(nc, sem, ps, v, identb, q_head, k_head, vals, q_rows, k_rows, o_rows,
                        den_rows)
        output_phase(nc, sem, ps, x, stats, woT, block_rows, o_rows, den_rows)
        norm_phase(nc, sem, "n3", ps, x, stats, xnT, ident, gateT, logits)
        routing_phase(nc, sem, "r3", ps, logits, rank, identb, combT)
        expert_phase(nc, sem, "e3", ps, x, xnT, wgate, wup, wdown, expert_rows, combT, ident,
                     out_dram=out_dram)


def load_phase(nc, sem, sb, g):
    ps, ident, raw_w = g["ps"], g["ident"], g["raw_w"]
    loaded = sem("ld_loaded")
    x_loaded = [sem(f"ld_x_loaded{i}") for i in range(4)]
    w_loaded = [sem("ld_" + w) for w in ("wgate", "wup", "wdown")]
    rounded = sem("ld_rounded")
    consts = sem("ld_consts")
    filled = sem("ld_filled")
    turned = sem("ld_turned")
    copied = sem("ld_copied")
    lows = sem("ld_lows")
    with ExitStack() as tmp:
        def tb(name, shape, dt=F32):
            return tmp.enter_context(nc.sbuf_tensor(name, shape, dt))
        raw = tb("ld_raw", [P, 4, D])
        raw_gate = tb("ld_gate", [E + 1, D])
        raw_rope = tb("ld_rope", [P, 2, TPB, HD // 2])
        ropeT = tb("ld_ropeT", [HD // 2, 2, BLK])
        rows32 = tb("ld_rows32", [3 * (E + 1), CH * P])
        dim_rows = tb("ld_dim_rows", [HD, P])
        pair_rows = tb("ld_pair_rows", [HD // 2, 2, P])
        raw_nw = tb("ld_nw", [HD, 2])
        first_turned = P - (PATCH - (TPB - 1) * P)
        block = tmp.enter_context(nc.Block())

        @block.sync
        def _(sp):
            sp.dma_start(ident[:], g["c_ident"]).then_inc(consts, 16)
            for i, w in enumerate(("wq", "wk", "wv", "wo")):
                sp.dma_start(raw[:, i, :], g[w]).then_inc(consts, 16)
            sp.dma_start(raw_gate[0:E, :], g["gate_w"]).then_inc(consts, 16)
            sp.dma_start(raw_gate[E:E + 1, :], g["shared_gate_w"]).then_inc(consts, 16)
            sp.dma_start(dim_rows[:], g["c_dim_rows"]).then_inc(consts, 16)
            sp.dma_start(pair_rows[:], g["c_pair_rows"]).then_inc(consts, 16)
            sp.dma_start(raw_nw[:, 0:1], g["q_norm_w"].rearrange("(d a) -> d a", a=1)).then_inc(consts, 16)
            sp.dma_start(raw_nw[:, 1:2], g["k_norm_w"].rearrange("(d a) -> d a", a=1)).then_inc(consts, 16)
            sp.dma_start(rows32[:], g["c_expert_rows"]).then_inc(consts, 16)
            sp.wait_ge(filled, 2)
            for i, t in enumerate(("rope_cos", "rope_sin")):
                head = P - first_turned
                sp.dma_start(raw_rope[first_turned:P, i, 0, :], g[t][0:head, :]).then_inc(consts, 16)
                sp.dma_start(raw_rope[:, i, 1:TPB, :],
                             g[t][head:PATCH, :].rearrange("(n p) d -> p n d", p=P)).then_inc(consts, 16)
            sp.wait_ge(consts, 16 * 16)
            sp.wait_ge(loaded, 16 * 4)

        @block.gpsimd
        def _(pool):
            for i, (routed, shared) in enumerate((("w_gate", "sw_gate"), ("w_up", "sw_up"))):
                pool.dma_start(raw_w[i][:, 0:E * I].rearrange("h (e i) -> h e i", e=E),
                               g[routed].rearrange("e h i -> h e i")).then_inc(w_loaded[i], 16)
                pool.dma_start(raw_w[i][:, E * I:R], g[shared]).then_inc(w_loaded[i], 16)
            full = E * I // P
            assert full * P == E * I and (CH - full - 1) * P < I <= (CH - full) * P
            down = raw_w[2][:].rearrange("p (c d) -> p c d", c=CH)
            pool.dma_start(down[:, 0:full, :],
                           g["w_down"].rearrange("e i h -> (e i) h").rearrange("(c p) h -> p c h", p=P)).then_inc(w_loaded[2], 16)
            pool.dma_start(down[:, full, :], g["sw_down"][0:P, :]).then_inc(w_loaded[2], 16)
            pool.wait_ge(filled, 2)
            pool.dma_start(down[0:I - P, full + 1, :], g["sw_down"][P:I, :]).then_inc(w_loaded[2], 16)
            pool.dma_start(g["block_rows"][:], g["c_block_rows"]).then_inc(loaded, 16)
            pool.dma_start(g["head_mean"][:], g["c_head_mean"]).then_inc(loaded, 16)
            pool.dma_start(g["swap"][:], g["c_swap"]).then_inc(loaded, 16)
            pool.dma_start(g["rank"][:], g["c_rank"]).then_inc(loaded, 16)

        @block.scalar
        def _(act):
            n = NT // 4
            for i in range(4):
                act.dma_start(g["x"][:, i * n:(i + 1) * n, :],
                              g["x_dram"][:, i * n:(i + 1) * n, :]).then_inc(x_loaded[i], 16)
            act.wait_ge(filled, 2)
            for i, w in enumerate(("wgate", "wup", "wdown")):
                act.wait_ge(w_loaded[i], 16 * (2 if i < 2 else 3))
                hi = g[w][HI][:] if i < 2 else g[w][HI][:].rearrange("p c d -> p (c d)")
                act.activation(hi, raw_w[i][:], ACT.Copy).then_inc(rounded, 1)

        @block.tensor
        def _(pe):
            pe.wait_ge(consts, 16 * 16)
            for i in range(4):
                pe.transpose(ps[:, i, 0:D], raw[:, i, :], ident[:]).then_inc(turned, 1)
            pe.transpose(ps[:, 4, 0:E + 1], raw_gate[:], ident[0:E + 1, 0:E + 1]).then_inc(turned, 1)
            pe.matmul(ps[:, 5, 0:2], dim_rows[:], raw_nw[:], start=True, stop=True).then_inc(turned, 1)
            for i in range(2):
                for n in range(TPB):
                    last = pe.transpose(ps[0:HD // 2, 6 + i, n * P:(n + 1) * P], raw_rope[:, i, n, :], ident[:])
                last.then_inc(turned, 1)
            pe.wait_ge(lows, 4)
            for i in range(2):
                pe.wait_ge(copied, 7 + i)
                pe.matmul(ps[:, i, :], pair_rows[:, i, :], ropeT[:, i, :], start=True, stop=True).then_inc(turned, 1)

        @block.vector
        def _(dve):
            dve.memset(raw_w[0][:, R:], 0.0)
            dve.memset(raw_w[1][:, R:], 0.0)
            dve.memset(raw_w[2][32:64, (CH - 1) * P:], 0.0)
            dve.memset(raw_w[2][64:P, (CH - 1) * P:], 0.0)
            for part in g["gateT"]:
                dve.memset(part[:].bitcast(F32), 0.0)
            dve.memset(raw_rope[:, 0, :, :], 1.0).then_inc(filled, 1)
            dve.memset(raw_rope[:, 1, :, :], 0.0).then_inc(filled, 1)
            for i in range(BUFS):
                dve.memset(g["q_head"][i][:], 0.0)
                dve.memset(g["k_head"][i][:], 1.0)
                dve.memset(g["vals"][i][:, :, HD:HD1], 1.0)
                dve.memset(g["vals"][i][:, :, HD1:32], 0.0)
            dve.wait_ge(turned, 6)
            small = [(g[w], ps[:, i, 0:D]) for i, w in enumerate(("wqT", "wkT", "wvT"))]
            small.append((g["gateT"], ps[:, 4, 0:E + 1]))
            for parts, made in small:
                dve.tensor_copy(parts[HI][:, 0:made.shape[-1]], made).then_inc(copied, 1)
            dve.tensor_copy(g["woT"][:], ps[:, 3, 0:D]).then_inc(copied, 1)
            dve.tensor_scalar(g["norm_w"][:, 0:1], ps[:, 5, 0:1], float(HD) ** -0.5, None, ALU.mult).then_inc(copied, 1)
            for i in range(2):
                dve.wait_ge(turned, 7 + i)
                dve.tensor_copy(ropeT[:, i, :], ps[0:HD // 2, 6 + i, :]).then_inc(copied, 1)
            dve.wait_ge(copied, 4)
            for parts, made in small:
                n = made.shape[-1]
                dve.tensor_tensor(parts[LO][:, 0:n], made, parts[HI][:, 0:n].bitcast(F32), ALU.subtract).then_inc(lows, 1)
            dve.tensor_copy(g["norm_w"][:, 1:2], ps[:, 5, 1:2])
            dve.tensor_copy(g["identb"][:], ident[:])
            dve.tensor_copy(g["expert_rows"][:], rows32[:])
            for i in range(2):
                dve.wait_ge(turned, 9 + i)
                dve.tensor_copy(g["rope"][:, i, :], ps[:, i, :])
            for n in range(NT):
                if n % (NT // 4) == 0:
                    dve.wait_ge(x_loaded[n // (NT // 4)], 16)
                dve.bn_stats(g["stats"][:, n, :], g["x"][:, n, :])


def norm_phase(nc, sem, tag, ps, x, stats, xnT, ident, gateT=None, logits=None,
               split=()):
    step = sem(tag + "_step")
    rooted = sem(tag + "_rooted")
    normed = sem(tag + "_normed")
    turned = sem(tag + "_turned")
    rounded = sem(tag + "_rounded")
    rest = sem(tag + "_rest")
    scored = sem(tag + "_scored")
    scored_kept = sem(tag + "_scored_kept")
    back = sem(tag + "_back")
    kept = sem(tag + "_kept")
    TURNED, SCORED, BACK, BANKS = 0, 3, 5, 3
    NE = E + 1
    with ExitStack() as tmp:
        def tb(name, shape):
            return tmp.enter_context(nc.sbuf_tensor(f"{tag}_{name}", shape, F32))
        total = tb("total", [P, NT])
        diff = tb("diff", [P, NT])
        within = tb("within", [P, NT])
        mean = tb("mean", [P, NT])
        between = tb("between", [P, NT])
        spread = tb("spread", [P, NT])
        var = tb("var", [P, NT])
        std = tb("std", [P, NT])
        rstd = tb("rstd", [P, NT])
        xn = tb("xn", [P, 2, TPB, D])
        scoresT = tb("scoresT", [NE, 2, BLK])
        block = tmp.enter_context(nc.Block())

        @block.vector
        def _(dve):
            even, odd = stats[:, :, 0:3], stats[:, :, 3:6]
            dve.tensor_tensor(total[:], even[:, :, 1], odd[:, :, 1], ALU.add).then_inc(step, 1)
            dve.tensor_tensor(diff[:], even[:, :, 1], odd[:, :, 1], ALU.subtract).then_inc(step, 1)
            dve.tensor_tensor(within[:], even[:, :, 2], odd[:, :, 2], ALU.add).then_inc(step, 1)
            dve.wait_ge(step, 3)
            dve.scalar_tensor_tensor(between[:], diff[:], 0.25, diff[:], ALU.mult, ALU.mult).then_inc(step, 1)
            dve.tensor_scalar(spread[:], within[:], 1.0 / D, LN_EPS, ALU.mult, ALU.add).then_inc(step, 1)
            dve.tensor_scalar(mean[:], total[:], 0.5, None, ALU.mult).then_inc(step, 1)
            dve.wait_ge(step, 6)
            dve.tensor_tensor(var[:], between[:], spread[:], ALU.add).then_inc(step, 1)
            dve.wait_ge(rooted, 1)
            dve.reciprocal(rstd[:], std[:]).then_inc(step, 1)
            dve.wait_ge(step, 8)

            def low(b):
                dve.wait_ge(rounded, b + 1)
                cols = slice(b * BLK, (b + 1) * BLK)
                dve.tensor_tensor(xnT[LO][:, cols], ps[:, TURNED + b % BANKS, :], xnT[HI][:, cols].bitcast(F32),
                                  ALU.subtract).then_inc(rest, 1)

            for b in range(NB):
                if b >= 2:
                    dve.wait_ge(turned, b - 1)
                for j in range(TPB):
                    n = b * TPB + j
                    last = dve.tensor_scalar(xn[:, b % 2, j, :], x[:, n, :], mean[:, n:n + 1], rstd[:, n:n + 1],
                                             ALU.subtract, ALU.mult)
                last.then_inc(normed, 1)
                if b >= 1:
                    low(b - 1)
            low(NB - 1)

        @block.tensor
        def _(pe):
            def route(b):
                pe.wait_ge(rest, b + 1)
                if b >= 2:
                    pe.wait_ge(scored_kept, b - 1)
                for n, (wp, xp) in enumerate(PASSES):
                    last = pe.matmul(ps[:, SCORED + b % 2, :], gateT[wp][:], xnT[xp][:, b * BLK:(b + 1) * BLK],
                                     start=(n == 0), stop=(n == len(PASSES) - 1))
                last.then_inc(scored, 1)

            def turn_back(b):
                pe.wait_ge(scored_kept, b + 1)
                if b >= 2:
                    pe.wait_ge(kept, b - 1)
                for j in range(TPB):
                    last = pe.transpose(ps[:, BACK + b % 2, j * NE:(j + 1) * NE], scoresT[:, b % 2, j * P:(j + 1) * P],
                                        ident[0:NE, 0:NE])
                last.then_inc(back, 1)

            for b in range(NB + 4):
                if b < NB:
                    pe.wait_ge(normed, b + 1)
                    if b >= BANKS:
                        pe.wait_ge(rest, b - BANKS + 1)
                    for j in range(TPB):
                        last = pe.transpose(ps[:, TURNED + b % BANKS, j * P:(j + 1) * P], xn[:, b % 2, j, :], ident[:])
                    last.then_inc(turned, 1)
                if gateT is not None and 2 <= b < NB + 2:
                    route(b - 2)
                if gateT is not None and b >= 4:
                    turn_back(b - 4)

        @block.scalar
        def _(act):
            act.wait_ge(step, 7)
            act.activation(std[:], var[:], ACT.Sqrt).then_inc(rooted, 1)
            for b in range(NB + 4):
                if b < NB:
                    act.wait_ge(turned, b + 1)
                    act.activation(xnT[HI][:, b * BLK:(b + 1) * BLK], ps[:, TURNED + b % BANKS, :], ACT.Copy).then_inc(rounded, 1)
                if gateT is not None and 2 <= b < NB + 2:
                    n = b - 2
                    act.wait_ge(scored, n + 1)
                    if n >= 2:
                        act.wait_ge(back, n - 1)
                    act.activation(scoresT[:, n % 2, :], ps[0:NE, SCORED + n % 2, :], ACT.Copy).then_inc(scored_kept, 1)
                if gateT is not None and b >= 4:
                    n = b - 4
                    act.wait_ge(back, n + 1)
                    act.activation(logits[:, n * TPB:(n + 1) * TPB, :],
                                   ps[:, BACK + n % 2, 0:TPB * NE].rearrange("p (n e) -> p n e", e=NE),
                                   ACT.Copy).then_inc(kept, 1)

        if split:
            @block.gpsimd
            def _(pool):
                for raw, parts in split:
                    hi, lo = (a[:] if len(a.shape) == 2 else a[:].rearrange("p c d -> p (c d)") for a in parts)
                    pool.tensor_tensor(lo, raw[:], hi.bitcast(F32), ALU.subtract)


def routing_phase(nc, sem, tag, ps, logits, rank, identb, combT):
    step = sem(tag + "_step")
    shifted = sem(tag + "_shifted")
    exped = sem(tag + "_exped")
    split = sem(tag + "_split")
    turned = sem(tag + "_turned")
    kept = sem(tag + "_kept")
    NE = E + 1
    with ExitStack() as tmp:
        def tb(name, shape, dt=F32):
            return tmp.enter_context(nc.sbuf_tensor(f"{tag}_{name}", shape, dt))
        ex = tb("ex", [P, NT, E])
        ex9 = tb("ex9", [P, NT, 1])
        prob = tb("prob", [P, NT, E])
        key = tb("key", [P, NT, E])
        first = tb("first", [P, NT, E])
        both = tb("both", [P, NT, E])
        rest = tb("rest", [P, NT, E])
        top = tb("top", [P, 6, NT])
        comb = tb("comb", [P, NT, NE])
        resid = tb("resid", [P, NT, NE])
        parts = tb("parts", [P, NT, 3, NE], BF16)
        block = tmp.enter_context(nc.Block())

        def wide(a):
            return a.unsqueeze(2).broadcast_to([P, NT, E])

        @block.vector
        def _(dve):
            count = [0]

            def then(ins):
                count[0] += 1
                ins.then_inc(step, 1)
                dve.wait_ge(step, count[0])

            lg = logits[:, :, 0:E]
            then(dve.tensor_reduce(top[:, 0, :], lg, AX.X, ALU.max))
            dve.tensor_tensor(ex[:], lg, wide(top[:, 0, :]), ALU.subtract).then_inc(shifted, 1)
            dve.wait_ge(exped, 2)
            then(dve.tensor_reduce(top[:, 1, :], ex[:], AX.X, ALU.add))
            then(dve.reciprocal(top[:, 2, :], top[:, 1, :]))
            then(dve.tensor_tensor(prob[:], ex[:], wide(top[:, 2, :]), ALU.mult))
            then(dve.tensor_reduce(top[:, 0, :], prob[:], AX.X, ALU.max))
            then(dve.tensor_tensor(key[:], prob[:], wide(top[:, 0, :]), ALU.is_equal))
            then(dve.tensor_tensor(key[:], key[:], rank[:].unsqueeze(1).broadcast_to([P, NT, E]), ALU.mult))
            then(dve.tensor_reduce(top[:, 3, :], key[:], AX.X, ALU.max))
            then(dve.tensor_tensor(first[:], key[:], wide(top[:, 3, :]), ALU.is_equal))
            then(dve.scalar_tensor_tensor(rest[:], first[:], -2.0, prob[:], ALU.mult, ALU.add))
            then(dve.tensor_reduce(top[:, 1, :], rest[:], AX.X, ALU.max))
            then(dve.tensor_tensor(key[:], rest[:], wide(top[:, 1, :]), ALU.is_equal))
            then(dve.tensor_tensor(key[:], key[:], rank[:].unsqueeze(1).broadcast_to([P, NT, E]), ALU.mult))
            then(dve.tensor_reduce(top[:, 3, :], key[:], AX.X, ALU.max))
            then(dve.tensor_tensor(both[:], key[:], wide(top[:, 3, :]), ALU.is_equal))
            then(dve.tensor_tensor(both[:], both[:], first[:], ALU.add))
            then(dve.tensor_tensor(top[:, 4, :], top[:, 0, :], top[:, 1, :], ALU.add))
            then(dve.reciprocal(top[:, 5, :], top[:, 4, :]))
            then(dve.tensor_tensor(both[:], both[:], prob[:], ALU.mult))
            then(dve.tensor_tensor(comb[:, :, 0:E], both[:], wide(top[:, 5, :]), ALU.mult))
            then(dve.tensor_scalar(ex9[:], ex9[:], 1.0, None, ALU.add))
            then(dve.reciprocal(comb[:, :, E:NE], ex9[:]))
            then(dve.tensor_copy(parts[:, :, 0, :], comb[:]))
            then(dve.tensor_tensor(resid[:], comb[:], parts[:, :, 0, :], ALU.subtract))
            then(dve.tensor_copy(parts[:, :, 1, :], resid[:]))
            dve.tensor_tensor(parts[:, :, 2, :], resid[:], parts[:, :, 1, :], ALU.subtract).then_inc(split, 1)

        @block.scalar
        def _(act):
            act.activation(ex9[:], logits[:, :, E:NE], ACT.Exp, scale=-1.0).then_inc(exped, 1)
            act.wait_ge(shifted, 1)
            act.activation(ex[:], ex[:], ACT.Exp).then_inc(exped, 1)
            for b in range(NB):
                act.wait_ge(turned, b + 1)
                act.activation(combT[:, b * BLK:(b + 1) * BLK],
                               ps[0:3 * NE, b % 2, :].bitcast(BF16)[:, 0:BLK], ACT.Copy).then_inc(kept, 1)

        @block.tensor
        def _(pe):
            pe.wait_ge(split, 1)
            for b in range(NB):
                if b >= 2:
                    pe.wait_ge(kept, b - 1)
                for j in range(TPB):
                    last = pe.transpose(ps[0:3 * NE, b % 2, :].bitcast(BF16)[:, j * P:(j + 1) * P],
                                        parts[:, b * TPB + j, :, :].rearrange("p a e -> p (a e)"), identb[:])
                last.then_inc(turned, 1)


def expert_phase(nc, sem, tag, ps, x, xnT, wgate, wup, wdown, expert_rows, combT, ident, stats=None,
                 out_dram=None):
    gated = sem(tag + "_gated")
    upped = sem(tag + "_upped")
    spread = sem(tag + "_spread")
    silued = sem(tag + "_silued")
    product = sem(tag + "_product")
    weighted = sem(tag + "_weighted")
    rounded = sem(tag + "_rounded")
    hidden_ready = sem(tag + "_hidden_ready")
    summed = sem(tag + "_summed")
    summed_kept = sem(tag + "_summed_kept")
    turned = sem(tag + "_turned")
    added = sem(tag + "_added")
    stored = sem(tag + "_stored")
    rows = [min(P, R - c * P) for c in range(CH)]
    SLOTS = 4
    fours = 2 * CH - 3 * (-2 * CH % SLOTS)
    slot = [n % SLOTS if n < fours else (n - fours) % 3 for n in range(2 * CH)]
    assert fours >= 0 and fours % SLOTS == 0
    with ExitStack() as tmp:
        def tb(name, shape, dt=F32):
            return tmp.enter_context(nc.sbuf_tensor(f"{tag}_{name}", shape, dt))
        silu = tb("silu", [P, 2, BLK])
        prod = tb("prod", [P, 2, BLK])
        full = tb("full", [P, 2, BLK])
        hidden = [tb("hidden" + part, [P, SLOTS, BLK], F32R) for part in ("_hi", "_lo")]
        yT = tb("yT", [P, BLK])
        block = tmp.enter_context(nc.Block())
        GATE, UP, SPREAD, Y, YT = 0, 2, 4, 6, 7

        def over_blocks(eng, first, turn):
            first()
            with eng.Fori(0, NB // 2 - 1) as it:
                for par in range(2):
                    turn(it * 2 + par, par, False)
            turn(NB - 2, 0, False)
            turn(NB - 1, 1, True)

        @block.tensor
        def _(pe):
            def up(blk, par, c):
                n, i, cols = blk * CH + c, (par + c) % 2, slice(c * P, (c + 1) * P)
                tokens = bass.ds(blk * BLK, BLK)
                if not (isinstance(n, int) and n < 2):
                    pe.wait_ge(weighted, n - 1)
                for bank, w, done in ((GATE, wgate, gated), (UP, wup, upped)):
                    for m, (wp, xp) in enumerate(PASSES):
                        last = pe.matmul(ps[:, bank + i, :], w[wp][:, cols], xnT[xp][:, tokens],
                                         start=(m == 0), stop=(m == len(PASSES) - 1))
                    last.then_inc(done, 1)
                pe.matmul(ps[:, SPREAD + i, :], expert_rows[:, cols], combT[:, tokens],
                          start=True, stop=True).then_inc(spread, 1)

            def down(blk, par, c):
                pe.wait_ge(hidden_ready, blk * CH + c + 1)
                if c == 0:
                    pe.wait_ge(summed_kept, blk + PRIME)
                at = slot[par * CH + c]
                for m, (wp, hp) in enumerate(PASSES):
                    last = pe.matmul(ps[:, Y, :], wdown[wp][0:rows[c], c, :], hidden[hp][0:rows[c], at, :],
                                     start=(c == 0 and m == 0), stop=(c == CH - 1 and m == len(PASSES) - 1))
                if c == CH - 1:
                    last.then_inc(summed, 1)

            def first():
                for c in range(3):
                    up(0, 0, c)
                down(0, 0, 0)

            def turn(blk, par, last):
                for c in range(3, CH + 3):
                    if c < CH:
                        up(blk, par, c)
                    elif not last:
                        up(blk + 1, 1 - par, c - CH)
                    if c - 2 < CH:
                        down(blk, par, c - 2)
                    elif not last:
                        down(blk + 1, 1 - par, c - 2 - CH)
                pe.wait_ge(summed_kept, blk + 1 + PRIME)
                pe.wait_ge(added, blk + PRIME)
                for j in range(TPB):
                    tr = pe.transpose(ps[:, YT, j * P:(j + 1) * P], yT[:, j * P:(j + 1) * P], ident[:])
                tr.then_inc(turned, 1)

            over_blocks(pe, first, turn)

        @block.scalar
        def _(act):
            def gate(blk, par, c):
                i = (par + c) % 2
                act.wait_ge(gated, blk * CH + c + 1)
                act.activation(silu[:, i, :], ps[:, GATE + i, :], ACT.Silu).then_inc(silued, 1)

            def round_hidden(blk, par, c):
                act.wait_ge(weighted, blk * CH + c + 1)
                act.activation(hidden[HI][:, slot[par * CH + c], :], full[:, (par + c) % 2, :], ACT.Copy).then_inc(rounded, 1)

            def first():
                gate(0, 0, 0)
                gate(0, 0, 1)
                round_hidden(0, 0, 0)

            def turn(blk, par, last):
                for c in range(1, CH + 1):
                    if c + 1 < CH:
                        gate(blk, par, c + 1)
                    elif not last:
                        gate(blk + 1, 1 - par, c + 1 - CH)
                    if c < CH:
                        round_hidden(blk, par, c)
                    elif not last:
                        round_hidden(blk + 1, 1 - par, 0)
                act.wait_ge(summed, blk + 1)
                act.activation(yT[:], ps[:, Y, :], ACT.Copy).then_inc(summed_kept, 1)

            prime(act, summed_kept)
            over_blocks(act, first, turn)

        @block.vector
        def _(dve):
            def weigh(blk, par, c):
                n, i = blk * CH + c, (par + c) % 2
                dve.wait_ge(silued, n + 1)
                dve.wait_ge(upped, n + 1)
                dve.tensor_tensor(prod[:, i, :], silu[:, i, :], ps[:, UP + i, :], ALU.mult).then_inc(product, 1)
                dve.wait_ge(product, n + 1)
                dve.wait_ge(spread, n + 1)
                if not (isinstance(n, int) and n < 2):
                    dve.wait_ge(hidden_ready, n - 1)
                dve.tensor_tensor(full[:, i, :], prod[:, i, :], ps[:, SPREAD + i, :], ALU.mult).then_inc(weighted, 1)

            def first():
                for c in range(3):
                    weigh(0, 0, c)

            def turn(blk, par, last):
                for c in range(3, CH + 3):
                    if c < CH:
                        weigh(blk, par, c)
                    elif not last:
                        weigh(blk + 1, 1 - par, c - CH)
                dve.wait_ge(turned, blk + 1)
                tiles = x[:, bass.ds(blk * TPB, TPB), :].rearrange("p n d -> p (n d)")
                dve.scalar_tensor_tensor(tiles, ps[:, YT, :], 0.5, tiles, ALU.mult, ALU.add).then_inc(added, 1)
                if stats is not None:
                    dve.wait_ge(added, blk + 1 + PRIME)
                    for j in range(TPB):
                        dve.bn_stats(stats[:, bass.ds(blk * TPB + j, 1), :].rearrange("p n s -> p (n s)"),
                                     x[:, bass.ds(blk * TPB + j, 1), :].rearrange("p n d -> p (n d)"))

            prime(dve, added)
            over_blocks(dve, first, turn)

        @block.gpsimd
        def _(pool):
            with pool.Fori(0, NB // 2) as it:
                for n2 in range(2 * CH):
                    pool.wait_ge(rounded, it * 2 * CH + n2 + 1)
                    pool.tensor_tensor(hidden[LO][:, slot[n2], :], full[:, n2 % 2, :],
                                       hidden[HI][:, slot[n2], :].bitcast(F32), ALU.subtract).then_inc(hidden_ready, 1)

        if out_dram is not None:
            @block.sync
            def _(sp):
                with sp.Fori(0, NB) as blk:
                    sp.wait_ge(added, blk + 1 + PRIME)
                    sp.dma_start(out_dram[:, bass.ds(blk * TPB, TPB), :],
                                 x[:, bass.ds(blk * TPB, TPB), :]).then_inc(stored, 16)
                sp.wait_ge(stored, 16 * NB)


def qkv_phase(nc, sem, ps, xnT, weights, norm_w, head_mean, block_rows, swap, rope, ident, v, q_rows,
              k_rows):
    projected = sem("qk_projected")
    v_projected = sem("qk_v_projected")
    v_kept = sem("qk_v_kept")
    squared = sem("qk_squared")
    meaned = sem("qk_meaned")
    eps_set = sem("qk_eps_set")
    rooted = sem("qk_rooted")
    inverted = sem("qk_inverted")
    turned = sem("qk_turned")
    turned_kept = sem("qk_turned_kept")
    spread = sem("qk_spread")
    spread_kept = sem("qk_spread_kept")
    normed = sem("qk_normed")
    swapped = sem("qk_swapped")
    cosed = sem("qk_cosed")
    sined = sem("qk_sined")
    roped = sem("qk_roped")
    part0 = sem("qk_part0")
    rest1 = sem("qk_rest1")
    part1 = sem("qk_part1")
    part2 = sem("qk_part2")
    stored = [sem(f"qk_stored{i}") for i in range(2)]
    turned_blocks = [b * BPS + BPS - 1 for b in range(BATCH)]
    ORDER = turned_blocks + [n for n in range(NB) if n not in turned_blocks]
    assert len(turned_blocks) <= 2
    QK, V, SWAP, MEAN, BACK = 0, 4, 5, 6, 7
    FACTORS = 2 * HEADS * TPB
    assert FACTORS == P and (BATCH, BPS) == (2, TPB)
    with ExitStack() as tmp:
        def tb(name, shape, dt=F32):
            return tmp.enter_context(nc.sbuf_tensor("qk_" + name, shape, dt))
        eps = tb("eps", [P, 1])
        sq = tb("sq", [P, 2, 2, BLK])
        root = tb("root", [P, FACTORS])
        inv = tb("inv", [P, FACTORS])
        invT = tb("invT", [FACTORS, P])
        rstd = tb("rstd", [P, 2, 2, BLK])
        qn = tb("qn", [P, 2, 2, BLK])
        left = tb("left", [P, 2, 2, BLK])
        parts = tb("parts", [P, 2, 2, 3, BLK], BF16)
        block = tmp.enter_context(nc.Block())

        @block.tensor
        def _(pe):
            def project(m):
                cols = ORDER[m] * BLK
                for i in range(2):
                    if m >= 2:
                        pe.wait_ge(normed, 2 * (m - 2) + i + 1)
                    for n, (wp, xp) in enumerate(PASSES):
                        last = pe.matmul(ps[:, QK + 2 * (m % 2) + i, :], weights[i][wp][:], xnT[xp][:, cols:cols + BLK],
                                         start=(n == 0), stop=(n == len(PASSES) - 1))
                    last.then_inc(projected, 1)

            def project_v(m):
                if m >= 1:
                    pe.wait_ge(v_kept, m)
                for j in range(TPB):
                    tokens = slice(ORDER[m] * BLK + j * P, ORDER[m] * BLK + (j + 1) * P)
                    for n, (xp, wp) in enumerate(PASSES):
                        last = pe.matmul(ps[:, V, j * D:(j + 1) * D], xnT[xp][:, tokens], weights[2][wp][:],
                                         start=(n == 0), stop=(n == len(PASSES) - 1))
                last.then_inc(v_projected, 1)

            def mean(m):
                if m >= 1:
                    pe.wait_ge(rooted, m)
                for i in range(2):
                    pe.wait_ge(squared, 2 * m + i + 1)
                    for j in range(TPB):
                        at = (i * TPB + j) * HEADS
                        last = pe.matmul(ps[:, MEAN, at:at + HEADS], sq[:, m % 2, i, j * P:(j + 1) * P], head_mean[:],
                                         start=True, stop=True)
                last.then_inc(meaned, 1)

            def spread_back(m, i):
                pe.wait_ge(turned_kept, m + 1)
                if m or i:
                    pe.wait_ge(spread_kept, 2 * m + i)
                for j in range(TPB):
                    last = pe.matmul(ps[:, BACK, j * P:(j + 1) * P], block_rows[:, i * TPB + j, :], invT[:],
                                     start=True, stop=True)
                last.then_inc(spread, 1)

            def turn_factors(m):
                pe.wait_ge(inverted, m + 1)
                pe.transpose(ps[:, MEAN, FACTORS:2 * FACTORS], inv[:], ident[:]).then_inc(turned, 1)

            def exchange(m):
                for i in range(2):
                    pe.wait_ge(normed, 2 * m + i + 1)
                    if m or i:
                        pe.wait_ge(sined, 2 * m + i)
                    pe.matmul(ps[:, SWAP, :], swap[:], qn[:, m % 2, i, :], start=True, stop=True).then_inc(swapped, 1)

            for m in range(NB + 1):
                if m < NB:
                    project(m)
                if m >= 1:
                    turn_factors(m - 1)
                if m < NB:
                    project_v(m)
                if m >= 1:
                    spread_back(m - 1, 0)
                if m < NB:
                    mean(m)
                if m >= 1:
                    spread_back(m - 1, 1)
                if 1 <= m < 1 + len(turned_blocks):
                    exchange(m - 1)

        @block.scalar
        def _(act):
            def keep_spread(m, i):
                act.wait_ge(spread, 2 * m + i + 1)
                act.activation(rstd[:, m % 2, i, :], ps[:, BACK, :], ACT.Copy).then_inc(spread_kept, 1)

            act.wait_ge(eps_set, 1)
            for m in range(NB + 1):
                if m < NB:
                    for i in range(2):
                        act.wait_ge(projected, 2 * m + i + 1)
                        act.activation(sq[:, m % 2, i, :], ps[:, QK + 2 * (m % 2) + i, :], ACT.Square).then_inc(squared, 1)
                if m >= 1:
                    act.wait_ge(turned, m)
                    if m >= 2:
                        act.wait_ge(spread, 2 * (m - 1))
                    act.activation(invT[:], ps[:, MEAN, FACTORS:2 * FACTORS], ACT.Copy).then_inc(turned_kept, 1)
                if m < NB:
                    act.wait_ge(v_projected, m + 1)
                    b, n = divmod(ORDER[m], BPS)
                    act.activation(v[:, b, :, n * TPB:(n + 1) * TPB, :].rearrange("p h t d -> p t h d"),
                                   ps[:, V, :].rearrange("p (t h d) -> p t h d", t=TPB, h=HEADS),
                                   ACT.Copy).then_inc(v_kept, 1)
                if m >= 1:
                    keep_spread(m - 1, 0)
                if m < NB:
                    act.wait_ge(meaned, m + 1)
                    if m >= 1:
                        act.wait_ge(inverted, m)
                    act.activation(root[:].rearrange("p (i h j) -> p i h j", i=2, h=HEADS),
                                   ps[:, MEAN, 0:FACTORS].rearrange("p (i j h) -> p i h j", i=2, j=TPB),
                                   ACT.Sqrt, bias=eps[:]).then_inc(rooted, 1)
                if m >= 1:
                    keep_spread(m - 1, 1)
                if m >= 1:
                    for i in range(2):
                        done = roped if m - 1 < len(turned_blocks) else normed
                        act.wait_ge(done, 2 * (m - 1) + i + 1)
                        if m >= 3:
                            act.wait_ge(stored[(m - 1) % 2], 16 * 2 * ((m - 1) // 2))
                        act.activation(parts[:, (m - 1) % 2, i, 0, :], qn[:, (m - 1) % 2, i, :], ACT.Copy).then_inc(part0, 1)

        @block.vector
        def _(dve):
            def invert(m):
                dve.wait_ge(rooted, m + 1)
                if m >= 1:
                    dve.wait_ge(turned, m)
                dve.reciprocal(inv[:], root[:]).then_inc(inverted, 1)

            dve.memset(eps[:], RMS_EPS).then_inc(eps_set, 1)
            invert(0)
            for m in range(NB):
                par = m % 2
                for i in range(2):
                    dve.wait_ge(spread_kept, 2 * m + i + 1)
                    dve.scalar_tensor_tensor(qn[:, par, i, :], ps[:, QK + 2 * par + i, :], norm_w[:, i:i + 1],
                                             rstd[:, par, i, :], ALU.mult, ALU.mult).then_inc(normed, 1)
                if m < len(turned_blocks):
                    for i in range(2):
                        dve.wait_ge(normed, 2 * m + i + 1)
                        dve.tensor_tensor(left[:, par, i, :], qn[:, par, i, :], rope[:, 0, :], ALU.mult).then_inc(cosed, 1)
                    for i in range(2):
                        dve.wait_ge(swapped, 2 * m + i + 1)
                        dve.tensor_tensor(rstd[:, par, i, :], ps[:, SWAP, :], rope[:, 1, :], ALU.mult).then_inc(sined, 1)
                    for i in range(2):
                        dve.wait_ge(cosed, 2 * m + i + 1)
                        dve.wait_ge(sined, 2 * m + i + 1)
                        dve.tensor_tensor(qn[:, par, i, :], left[:, par, i, :], rstd[:, par, i, :],
                                          ALU.add).then_inc(roped, 1)
                if m < NB - 1:
                    invert(m + 1)
                for i in range(2):
                    dve.wait_ge(part0, 2 * m + i + 1)
                    dve.tensor_tensor(left[:, par, i, :], qn[:, par, i, :], parts[:, par, i, 0, :],
                                      ALU.subtract).then_inc(rest1, 1)
                for i in range(2):
                    dve.wait_ge(rest1, 2 * m + i + 1)
                    dve.tensor_copy(parts[:, par, i, 1, :], left[:, par, i, :]).then_inc(part1, 1)

        @block.gpsimd
        def _(pool):
            for m in range(NB):
                for i in range(2):
                    pool.wait_ge(part1, 2 * m + i + 1)
                    pool.tensor_tensor(parts[:, m % 2, i, 2, :], left[:, m % 2, i, :], parts[:, m % 2, i, 1, :],
                                       ALU.subtract).then_inc(part2, 1)

        @block.sync
        def _(sp):
            for m in range(NB):
                b, n = divmod(ORDER[m], BPS)
                for i, rows in enumerate((q_rows, k_rows)):
                    sp.wait_ge(part2, 2 * m + i + 1)
                    heads = rows[b * HEADS:(b + 1) * HEADS, :, :, n * BLK:(n + 1) * BLK]
                    sp.dma_start(heads.rearrange("h d j t -> (h d) j t"), parts[:, m % 2, i, :, :]).then_inc(stored[m % 2], 16)
            for i in range(2):
                sp.wait_ge(stored[i], 16 * NB)


def attention_phase(nc, sem, ps, v, identb, q, k, vals, q_rows, k_rows, o_rows, den_rows):
    CHUNKS = SEQ // BLK
    STEPS = KT * CHUNKS
    AHEAD, LAG = 2, 11
    TURNS = BH - AHEAD
    assert TURNS % BUFS == 0 and STEPS % BUFS == 1
    qk_loaded = [sem(f"at_qk_loaded{i}") for i in range(BUFS)]
    max_scored = sem("at_max_scored")
    max_reduced = sem("at_max_reduced")
    max_step = sem("at_max_step")
    max_turned = sem("at_max_turned")
    max_kept = sem("at_max_kept")
    max_placed = sem("at_max_placed")
    scored = sem("at_scored")
    exped = sem("at_exped")
    weighed = sem("at_weighed")
    values_placed = sem("at_values_placed")
    sums_kept = sem("at_sums_kept")
    sums_stored = sem("at_sums_stored")
    SUM_DMAS, LOAD_DMAS = 2 * CHUNKS, 6
    assert PAIRS == [(a, b) for a in range(3) for b in range(3 - a)]
    VSTEPS = 5
    with ExitStack() as tmp:
        def tb(name, shape, dt=F32):
            return tmp.enter_context(nc.sbuf_tensor("at_" + name, shape, dt))
        prob = tb("prob", [P, PROBS, CHUNKS, BLK])
        mx = tb("mx", [P, KT, CHUNKS])
        neg = tb("neg", [P, KT])
        res = tb("res", [P, KT])
        mparts = tb("mparts", [P, MR, KT], BF16)
        mrows = tb("mrows", [MR * KT, P], BF16)
        sums = tb("sums", [P, BLK])
        block = tmp.enter_context(nc.Block())
        S, M, O, X = 0, 3, 6, 7

        @block.gpsimd
        def _(pool):
            def place(h, i):
                head = v[:].rearrange("p b h t d -> p (b h) t d")[:, h, :, :]
                pool.tensor_copy(vals[i][:, :, 0:HD], head).then_inc(values_placed, 1)

            for i in range(BUFS):
                place(i, i)

            def replace(h, i):
                pool.wait_ge(weighed, (h + 1) * KT + PRIME)
                place(h + BUFS, i)

            with pool.Fori(0, BH // BUFS - 1) as it:
                for i in range(BUFS):
                    replace(it * BUFS + i, i)
            for h in range((BH // BUFS - 1) * BUFS, BH - BUFS):
                replace(h, h % BUFS)

        @block.sync
        def _(sp):
            def load(h, i):
                for part in range(3):
                    first = PAIRS.index((part, 0))
                    times = 3 - part
                    rows = slice(first * HD, (first + times) * HD)
                    same = q_rows[h][:, part, :].unsqueeze(0).broadcast_to([times, HD, SEQ])
                    sp.dma_start(q[i][rows, :], same).then_inc(qk_loaded[i], 16)
                    sp.dma_start(k[i][rows, :], k_rows[h][:, 0:times, :].rearrange("d j t -> j d t")).then_inc(qk_loaded[i], 16)

            def place_maxima(h, i):
                sp.wait_ge(max_kept, h + 1)
                sp.dma_start(q[i][MROW:MROW + MR, :], mrows[:]).then_inc(max_placed, 16)

            def store_sums(h):
                sp.wait_ge(sums_kept, h + 1 + PRIME)
                for c in range(CHUNKS):
                    cols = slice(c * BLK, (c + 1) * BLK)
                    sp.dma_start(o_rows[h][:, cols], sums[32 * c:32 * c + HD, :]).then_inc(sums_stored, 16)
                    sp.dma_start(den_rows[h][:, cols], sums[32 * c + HD:32 * c + HD1, :]).then_inc(sums_stored, 16)

            def turn(h, i):
                place_maxima(h + 1, (i + 1) % BUFS)
                sp.wait_ge(weighed, (h + 1) * KT + PRIME)
                load(h + BUFS, i)
                store_sums(h)

            prime(sp, sums_stored)
            for h in range(BUFS):
                load(h, h)
            place_maxima(0, 0)
            with sp.Fori(0, BH // BUFS - 1) as it:
                for i in range(BUFS):
                    turn(it * BUFS + i, i)
            for h in range((BH // BUFS - 1) * BUFS, BH):
                if h < BH - BUFS:
                    turn(h, h % BUFS)
                else:
                    if h < BH - 1:
                        place_maxima(h + 1, (h + 1) % BUFS)
                    store_sums(h)
            sp.wait_ge(sums_stored, 16 * SUM_DMAS * BH + PRIME)

        @block.scalar
        def _(act):
            def exps(h, i, g):
                for c in range(CHUNKS):
                    n = h * STEPS + g * CHUNKS + c
                    act.wait_ge(scored, n + 1)
                    act.activation(prob[:, g % PROBS, c, :], ps[:, S + (i + g * CHUNKS + c) % BUFS, :],
                                   ACT.Exp).then_inc(exped, 1)

            def keep_sums(h):
                act.wait_ge(weighed, (h + 1) * KT + PRIME)
                act.wait_ge(sums_stored, 16 * SUM_DMAS * h + PRIME)
                act.activation(sums[:], ps[:, O, :], ACT.Copy).then_inc(sums_kept, 1)

            def keep_maxima(h):
                act.wait_ge(max_turned, h + 1 + PRIME)
                if not (isinstance(h, int) and h == 0):
                    act.wait_ge(max_placed, 16 * h)
                act.activation(mrows[:], ps[0:MR * KT, X, 0:P], ACT.Copy).then_inc(max_kept, 1)

            def turn(h, i, last=False):
                for g in range(1, KT):
                    if not (isinstance(h, int) and h == 0 and g < PROBS):
                        act.wait_ge(weighed, h * KT + max(g - PROBS, -1) + 1 + PRIME)
                    exps(h, i, g)
                    if g == LAG + 2 and not last:
                        keep_maxima(h + 1)
                if not last:
                    act.wait_ge(weighed, (h + 1) * KT - PROBS + 1 + PRIME)
                    exps(h + 1, i + 1, 0)
                keep_sums(h)

            prime(act, sums_kept)
            keep_maxima(0)
            exps(0, 0, 0)
            with act.Fori(0, TURNS // BUFS) as it:
                for i in range(BUFS):
                    turn(it * BUFS + i, i)
            turn(BH - 2, (BH - 2) % BUFS)
            turn(BH - 1, (BH - 1) % BUFS, last=True)

        @block.tensor
        def _(pe):
            def maxima(h, i, j):
                n, c = h * STEPS + j, j % CHUNKS
                if not (isinstance(n, int) and n < BUFS):
                    pe.wait_ge(max_reduced, n - BUFS + 1)
                pe.matmul(ps[:, M + (i + j) % BUFS, :], q[i][0:MROW, (j // CHUNKS) * P:(j // CHUNKS + 1) * P],
                          k[i][0:MROW, c * BLK:(c + 1) * BLK], start=True, stop=True).then_inc(max_scored, 1)

            def turn_maxima(h):
                pe.wait_ge(max_step, (h + 1) * VSTEPS)
                pe.matmul(ps[0:MR * KT, X, 0:P], mparts[:].rearrange("p a t -> p (a t)"), identb[:],
                          start=True, stop=True).then_inc(max_turned, 1)

            def scores(h, i, g, c):
                n = h * STEPS + g * CHUNKS + c
                if not (isinstance(n, int) and n < BUFS):
                    pe.wait_ge(exped, n - BUFS + 1)
                pe.matmul(ps[:, S + (i + g * CHUNKS + c) % BUFS, :], k[i][:, g * P:(g + 1) * P],
                          q[i][:, c * BLK:(c + 1) * BLK], start=True, stop=True).then_inc(scored, 1)

            def weigh(h, i, g):
                pe.wait_ge(exped, h * STEPS + (g + 1) * CHUNKS)
                if g == 0:
                    pe.wait_ge(values_placed, h + 1)
                    pe.wait_ge(sums_kept, h + PRIME)
                for c in range(CHUNKS):
                    last = pe.matmul(ps[32 * c:32 * c + 32, O, :], vals[i][:, g, :], prob[:, g % PROBS, c, :],
                                     start=(g == 0), stop=(g == KT - 1), skip_group_check=True)
                last.then_inc(weighed, 1)

            def turn(h, i, loads=None, last=False):
                nxt, far = (i + 1) % BUFS, (i + AHEAD) % BUFS
                for g in range(1, KT + 1):
                    if g == LAG + 1 and loads is not None:
                        pe.wait_ge(qk_loaded[far], 16 * LOAD_DMAS * loads)
                    if g == KT and not last:
                        pe.wait_ge(max_placed, 16 * (h + 2))
                    for c in range(CHUNKS):
                        if g < KT:
                            scores(h, i, g, c)
                        elif not last:
                            scores(h + 1, nxt, 0, c)
                        if g <= LAG and not last:
                            maxima(h + 1, nxt, (KT - LAG + g - 1) * CHUNKS + c)
                        elif g > LAG and loads is not None:
                            maxima(h + AHEAD, far, (g - LAG - 1) * CHUNKS + c)
                    weigh(h, i, g - 1)
                    if g == LAG + 1 and not last:
                        turn_maxima(h + 1)

            prime(pe, weighed, max_turned)
            for h in range(AHEAD):
                pe.wait_ge(qk_loaded[h], 16 * LOAD_DMAS)
                for j in range(STEPS if h == 0 else (KT - LAG) * CHUNKS):
                    maxima(h, h, j)
                if h == 0:
                    turn_maxima(0)
            pe.wait_ge(max_placed, 16)
            for c in range(CHUNKS):
                scores(0, 0, 0, c)
            with pe.Fori(0, TURNS // BUFS) as it:
                for i in range(BUFS):
                    turn(it * BUFS + i, i, loads=it + 1 + (i + AHEAD) // BUFS)
            turn(BH - 2, (BH - 2) % BUFS)
            turn(BH - 1, (BH - 1) % BUFS, last=True)

        @block.vector
        def _(dve):
            def maxima(h, i):
                for j in range(STEPS):
                    dve.wait_ge(max_scored, h * STEPS + j + 1)
                    dve.tensor_reduce(mx[:, j // CHUNKS, j % CHUNKS:j % CHUNKS + 1], ps[:, M + (i + j) % BUFS, :],
                                      AX.X, ALU.max).then_inc(max_reduced, 1)
                at = h * VSTEPS
                dve.wait_ge(max_reduced, h * STEPS + STEPS)
                dve.tensor_reduce(neg[:], mx[:], AX.X, ALU.max, negate=True).then_inc(max_step, 1)
                dve.wait_ge(max_step, at + 1)
                dve.wait_ge(max_turned, h + PRIME)
                dve.tensor_copy(mparts[:, 0, :], neg[:]).then_inc(max_step, 1)
                dve.wait_ge(max_step, at + 2)
                dve.tensor_tensor(res[:], neg[:], mparts[:, 0, :], ALU.subtract).then_inc(max_step, 1)
                dve.wait_ge(max_step, at + 3)
                dve.tensor_copy(mparts[:, 1, :], res[:]).then_inc(max_step, 1)
                dve.wait_ge(max_step, at + 4)
                dve.tensor_tensor(mparts[:, 2, :], res[:], mparts[:, 1, :], ALU.subtract).then_inc(max_step, 1)

            with dve.Fori(0, TURNS // BUFS) as it:
                for i in range(BUFS):
                    maxima(it * BUFS + i, i)
            for h in range(TURNS, BH):
                maxima(h, h % BUFS)


def output_phase(nc, sem, ps, x, stats, woT, block_rows, o_rows, den_rows):
    den_loaded = sem("op_den_loaded")
    loaded = [sem(f"op_loaded{i}") for i in range(2)]
    inverted = sem("op_inverted")
    spread = sem("op_spread")
    divided = sem("op_divided")
    projected = sem("op_projected")
    added = sem("op_added")
    SPREAD, OUT = 0, 2
    assert BH * BPS == P
    with ExitStack() as tmp:
        def tb(name, shape):
            return tmp.enter_context(nc.sbuf_tensor("op_" + name, shape, F32))
        o = tb("o", [P, NB, BLK])
        den = tb("den", [P, BLK])
        inv = tb("inv", [P, BLK])
        oT = tb("oT", [P, 2, BLK])
        block = tmp.enter_context(nc.Block())

        def load(eng, blk):
            b, n = divmod(blk, BPS)
            eng.dma_start(o[:, blk, :], o_rows[b * HEADS:(b + 1) * HEADS, :, n * BLK:(n + 1) * BLK]).then_inc(loaded[blk % 2], 16)

        @block.sync
        def _(sp):
            sp.dma_start(den[:], den_rows.rearrange("h a (n t) -> (h a n) t", n=BPS)).then_inc(den_loaded, 16)
            for blk in range(0, NB, 2):
                load(sp, blk)
                sp.wait_ge(loaded[0], 16 * (blk // 2 + 1))

        @block.scalar
        def _(act):
            for blk in range(1, NB, 2):
                load(act, blk)
                act.wait_ge(loaded[1], 16 * (blk // 2 + 1))

        @block.vector
        def _(dve):
            dve.wait_ge(den_loaded, 16)
            dve.reciprocal(inv[:], den[:]).then_inc(inverted, 1)
            for blk in range(NB + 1):
                if blk < NB:
                    dve.wait_ge(loaded[blk % 2], 16 * (blk // 2 + 1))
                    dve.wait_ge(spread, blk + 1)
                    if blk >= 2:
                        dve.wait_ge(projected, blk - 1)
                    dve.tensor_tensor(oT[:, blk % 2, :], o[:, blk, :], ps[:, SPREAD + blk % 2, :], ALU.mult).then_inc(divided, 1)
                if blk >= 1:
                    n = blk - 1
                    dve.wait_ge(projected, n + 1)
                    tiles = x[:, n * TPB:(n + 1) * TPB, :].rearrange("p n d -> p (n d)")
                    dve.tensor_tensor(tiles, ps[:, OUT + n % 2, :], tiles, ALU.add).then_inc(added, 1)
                    dve.wait_ge(added, n + 1)
                    for j in range(n * TPB, (n + 1) * TPB):
                        dve.bn_stats(stats[:, j, :], x[:, j, :])

        @block.tensor
        def _(pe):
            pe.wait_ge(inverted, 1)
            for blk in range(NB + 1):
                if blk < NB:
                    if blk >= 2:
                        pe.wait_ge(divided, blk - 1)
                    pe.matmul(ps[:, SPREAD + blk % 2, :], block_rows[:, blk, :], inv[:], start=True, stop=True).then_inc(spread, 1)
                if blk >= 1:
                    n = blk - 1
                    pe.wait_ge(divided, n + 1)
                    if n >= 2:
                        pe.wait_ge(added, n - 1)
                    for j in range(TPB):
                        last = pe.matmul(ps[:, OUT + n % 2, j * D:(j + 1) * D], oT[:, n % 2, j * P:(j + 1) * P], woT[:],
                                         start=True, stop=True)
                    last.then_inc(projected, 1)


_INS = ["L0_attn_x", "L0_attn_rope_cos", "L0_attn_rope_sin", "L0_attn_wq", "L0_attn_wk", "L0_attn_wv",
        "L0_attn_wo", "L0_attn_q_norm_w", "L0_attn_k_norm_w", "L0_ffn_gate_w", "L0_ffn_w_gate",
        "L0_ffn_w_up", "L0_ffn_w_down", "L0_ffn_sw_gate", "L0_ffn_sw_up", "L0_ffn_sw_down",
        "L0_ffn_shared_gate_w"]


def _constants():
    import numpy as np

    row = np.arange(P)
    col = np.arange(CH * P)
    expert = np.tile(np.arange(E + 1), 3)
    return {
        "ident": np.eye(P, dtype=np.float32),
        "expert_rows": (expert[:, None] == col[None, :] // I).astype(np.float32),
        "block_rows": np.stack([row[:, None] == (b * HEADS + row[None, :] // HD) * BPS + n
                                for b in range(BATCH) for n in range(BPS)], axis=1).astype(np.float32),
        "dim_rows": (np.arange(HD)[:, None] == row[None, :] % HD).astype(np.float32),
        "pair_rows": np.stack([
            (np.arange(HD // 2)[:, None] == row[None, :] % HD // 2).astype(np.float32),
            (np.arange(HD // 2)[:, None] == row[None, :] % HD // 2) * np.where(row % 2 == 0, -1, 1).astype(np.float32),
        ], axis=1).astype(np.float32),
        "head_mean": (row[:, None] // HD == np.arange(HEADS)[None, :]).astype(np.float32) / HD,
        "swap": (row[:, None] == (row[None, :] ^ 1)).astype(np.float32),
        "rank": np.tile(np.arange(E, 0, -1, dtype=np.float32), (P, 1)),
    }


def kernel(**inputs):
    import numpy as _np
    import concourse.bacc as _bacc
    from concourse import mybir as _mybir
    from concourse.bass_utils import run_bass_kernel_spmd as _run

    nc = _bacc.Bacc("TRN2", target_bir_lowering=False, num_devices=1)
    arrays, args = {}, []
    for name in _INS:
        a = _np.ascontiguousarray(inputs[name])
        arrays[f"in_{name}_dram"] = a
        args.append(nc.dram_tensor(f"in_{name}_dram", a.shape, _mybir.dt.from_np(a.dtype), kind="ExternalInput").ap())
    for name, a in _constants().items():
        arrays[f"const_{name}_dram"] = a
        args.append(nc.dram_tensor(f"const_{name}_dram", a.shape, _mybir.dt.from_np(a.dtype), kind="ExternalInput").ap())
    args.append(nc.dram_tensor("out_0_dram", (BATCH, SEQ, D), F32, kind="ExternalOutput").ap())
    build(nc, *args)
    r = _run(nc, [arrays], core_ids=[0])
    return r.results[0]["out_0_dram"]
```

```python
from contextlib import ExitStack

import concourse.bass as bass
from concourse import mybir

F32 = mybir.dt.float32
F32R = mybir.dt.float32r
BF16 = mybir.dt.bfloat16
ALU = mybir.AluOpType
ACT = mybir.ActivationFunctionType
AX = mybir.AxisListType

P = 128
D = 128
BATCH, SEQ = 2, 2048
T = BATCH * SEQ
NT = T // P
BLK = 512
NB = T // BLK
TPB = BLK // P
BPS = SEQ // BLK
E = 8
I = 176
R = (E + 1) * I
CH = -(-R // P)
TAIL = R - (CH - 1) * P
TAIL_UP = P // 2
assert 0 < TAIL <= TAIL_UP and E * I <= (CH - 1) * P
HEADS, HD = 16, 8
HD1 = HD + 1
BH = BATCH * HEADS
PATCH = 508
KT = SEQ // P
LN_EPS, RMS_EPS = 1e-5, 1e-6
BUFS = 3
PROBS = 4
W_DMAS = (3, 2, 3)
PRIME = 1

PAIRS = [(0, 0), (0, 1), (0, 2), (1, 0), (1, 1), (2, 0)]
KR = len(PAIRS) * HD
MR = 3
MROW = 96


HI, LO = 0, 1
PASSES = [(HI, HI), (HI, LO), (LO, HI)]


def flat(a):
    return a[:] if len(a.shape) == 2 else a[:].rearrange("p c d -> p (c d)")


def prime(eng, *sems):
    for s in sems:
        eng.sem_inc(s, PRIME)


def build(nc, x_in, rope_cos, rope_sin, wq, wk, wv, wo, q_norm_w, k_norm_w, gate_w, w_gate, w_up,
          w_down, sw_gate, sw_up, sw_down, shared_gate_w, c_ident, c_expert_rows, c_block_rows,
          c_dim_rows, c_pair_rows, c_head_mean, c_swap, c_rank, out):
    x_dram = x_in.rearrange("b (n p) d -> p (b n) d", p=P)
    out_dram = out.rearrange("b (n p) d -> p (b n) d", p=P)
    q_rows = nc.dram_tensor("q_rows", (BH, HD, 3, SEQ), BF16).ap()
    k_rows = nc.dram_tensor("k_rows", (BH, HD, 3, SEQ), BF16).ap()
    sum_rows = nc.dram_tensor("sum_rows", (BH, HD1, SEQ), F32).ap()

    nc.disable_value_cache = True
    with ExitStack() as ctx:
        def sb(name, shape, dt=F32):
            return ctx.enter_context(nc.sbuf_tensor(name, shape, dt))

        def sem(name):
            return ctx.enter_context(nc.semaphore(name))

        ps = ctx.enter_context(nc.psum_tensor("ps", [P, 8, BLK], F32))

        x = sb("x", [P, NT, D])
        stats = sb("stats", [P, NT, 6])
        xnT = [sb("xnT" + part, [P, T], F32R) for part in ("_hi", "_lo")]
        wgate = [sb("wgate" + part, [P, CH * P], F32R) for part in ("_hi", "_lo")]
        wup = [sb("wup" + part, [P, CH * P], F32R) for part in ("_hi", "_lo")]
        wdown = [sb("wdown" + part, [P, CH, D], F32R) for part in ("_hi", "_lo")]
        ident = sb("ident", [P, P])
        identb = sb("identb", [P, P], BF16)
        expert_rows = sb("expert_rows", [3 * (E + 1), CH * P], BF16)
        block_rows = sb("block_rows", [P, NB, P])
        head_mean = sb("head_mean", [P, HEADS])
        swap = sb("swap", [P, P])
        rank = sb("rank", [P, E])
        gateT = [sb("gateT" + part, [P, P], F32R) for part in ("_hi", "_lo")]
        wqT = [sb("wqT" + part, [P, D], F32R) for part in ("_hi", "_lo")]
        wkT = [sb("wkT" + part, [P, D], F32R) for part in ("_hi", "_lo")]
        wvT = [sb("wvT" + part, [P, D], F32R) for part in ("_hi", "_lo")]
        woT = sb("woT", [P, D])
        norm_w = sb("norm_w", [P, 2])
        rope = sb("rope", [P, 2, BLK])
        logits = sb("logits", [P, NT, E + 1])
        combT = sb("combT", [3 * (E + 1), T], BF16)
        v = sb("v", [P, BATCH, HEADS, KT, HD])
        q_head = [sb(f"q_head{i}", [P, SEQ], BF16) for i in range(BUFS)]
        k_head = [sb(f"k_head{i}", [P, SEQ], BF16) for i in range(BUFS)]
        vals = [sb(f"vals{i}", [P, KT, 32]) for i in range(BUFS)]

        with ExitStack() as weights_ctx:
            raw_w = [weights_ctx.enter_context(nc.sbuf_tensor("raw_" + w, [P, CH * P], F32))
                     for w in ("wgate", "wup", "wdown")]
            w_loaded = [sem("ld_" + w) for w in ("wgate", "wup", "wdown")]
            loaded = sem("ld_loaded")
            load_phase(nc, sem, sb, locals())
            norm_phase(nc, sem, "n1", ps, x, stats, xnT, ident, gateT, logits,
                       weights=list(zip(raw_w, (wgate, wup, wdown), w_loaded, W_DMAS)),
                       late=(loaded, 16 * 4))
        routing_phase(nc, sem, "r1", ps, logits, rank, identb, combT)
        expert_phase(nc, sem, "e1", ps, x, xnT, wgate, wup, wdown, expert_rows, combT, ident,
                     stats=stats)
        norm_phase(nc, sem, "n2", ps, x, stats, xnT, ident)
        qk_loaded = [sem(f"qk_loaded{i}") for i in range(BUFS)]
        qk_stored = [sem(f"qk_stored{i}") for i in range(2)]
        qkv_phase(nc, sem, ps, xnT, (wqT, wkT, wvT), norm_w, head_mean, swap, rope, ident, v,
                  q_rows, k_rows, q_head, k_head, qk_loaded, qk_stored)
        with ExitStack() as sums_ctx:
            def kept(name, shape, dt=F32):
                return sums_ctx.enter_context(nc.sbuf_tensor("at_" + name, shape, dt))

            sums_stored = sem("sums_stored")
            o_loaded = [sem(f"o_loaded{b}") for b in range(BATCH)]
            inverted = sem("inverted")
            o, den, inv = attention_phase(nc, sem, kept, ps, v, identb, q_head, k_head, vals, q_rows,
                                          k_rows, qk_loaded, qk_stored, sum_rows, sums_stored,
                                          o_loaded, inverted)
            output_phase(nc, sem, ps, x, stats, woT, block_rows, sum_rows, sums_stored, o, den, inv,
                         o_loaded, inverted)
        norm_phase(nc, sem, "n3", ps, x, stats, xnT, ident, gateT, logits)
        routing_phase(nc, sem, "r3", ps, logits, rank, identb, combT)
        expert_phase(nc, sem, "e3", ps, x, xnT, wgate, wup, wdown, expert_rows, combT, ident,
                     out_dram=out_dram)


def load_phase(nc, sem, sb, g):
    ps, ident, raw_w = g["ps"], g["ident"], g["raw_w"]
    x_loaded = [sem(f"ld_x_loaded{i}") for i in range(4)]
    consts = sem("ld_consts")
    filled = sem("ld_filled")
    turned = sem("ld_turned")
    copied = sem("ld_copied")
    lows = sem("ld_lows")
    with ExitStack() as tmp:
        def tb(name, shape, dt=F32):
            return tmp.enter_context(nc.sbuf_tensor(name, shape, dt))
        raw = tb("ld_raw", [P, 4, D])
        raw_gate = tb("ld_gate", [E + 1, D])
        raw_rope = tb("ld_rope", [P, 2, TPB, HD // 2])
        ropeT = tb("ld_ropeT", [HD // 2, 2, BLK])
        rows32 = tb("ld_rows32", [3 * (E + 1), CH * P])
        dim_rows = tb("ld_dim_rows", [HD, P])
        pair_rows = tb("ld_pair_rows", [HD // 2, 2, P])
        raw_nw = tb("ld_nw", [HD, 2])
        first_turned = P - (PATCH - (TPB - 1) * P)
        block = tmp.enter_context(nc.Block())

        @block.sync
        def _(sp):
            sp.dma_start(ident[:], g["c_ident"]).then_inc(consts, 16)
            for i, w in enumerate(("wq", "wk", "wv", "wo")):
                sp.dma_start(raw[:, i, :], g[w]).then_inc(consts, 16)
            sp.dma_start(raw_gate[0:E, :], g["gate_w"]).then_inc(consts, 16)
            sp.dma_start(raw_gate[E:E + 1, :], g["shared_gate_w"]).then_inc(consts, 16)
            sp.dma_start(dim_rows[:], g["c_dim_rows"]).then_inc(consts, 16)
            sp.dma_start(pair_rows[:], g["c_pair_rows"]).then_inc(consts, 16)
            sp.dma_start(raw_nw[:, 0:1], g["q_norm_w"].rearrange("(d a) -> d a", a=1)).then_inc(consts, 16)
            sp.dma_start(raw_nw[:, 1:2], g["k_norm_w"].rearrange("(d a) -> d a", a=1)).then_inc(consts, 16)
            sp.dma_start(rows32[:], g["c_expert_rows"]).then_inc(consts, 16)
            sp.wait_ge(filled, 2)
            for i, t in enumerate(("rope_cos", "rope_sin")):
                head = P - first_turned
                sp.dma_start(raw_rope[first_turned:P, i, 0, :], g[t][0:head, :]).then_inc(consts, 16)
                sp.dma_start(raw_rope[:, i, 1:TPB, :],
                             g[t][head:PATCH, :].rearrange("(n p) d -> p n d", p=P)).then_inc(consts, 16)
            w_loaded, loaded = g["w_loaded"], g["loaded"]
            for i, (routed, shared) in enumerate((("w_gate", "sw_gate"), ("w_up", "sw_up"))):
                sp.dma_start(raw_w[i][:, 0:E * I].rearrange("h (e i) -> h e i", e=E),
                               g[routed].rearrange("e h i -> h e i")).then_inc(w_loaded[i], 16)
                sp.dma_start(raw_w[i][:, E * I:R], g[shared]).then_inc(w_loaded[i], 16)
            tail_up = (CH - 1) * P + TAIL_UP
            sp.dma_start(raw_w[0][:, tail_up:tail_up + TAIL], g["sw_up"][:, I - TAIL:I]).then_inc(w_loaded[0], 16)
            full = E * I // P
            assert full * P == E * I and (CH - full - 1) * P < I <= (CH - full) * P
            down = raw_w[2][:].rearrange("p (c d) -> p c d", c=CH)
            sp.dma_start(down[:, 0:full, :],
                           g["w_down"].rearrange("e i h -> (e i) h").rearrange("(c p) h -> p c h", p=P)).then_inc(w_loaded[2], 16)
            sp.dma_start(down[:, full, :], g["sw_down"][0:P, :]).then_inc(w_loaded[2], 16)
            sp.dma_start(down[0:I - P, full + 1, :], g["sw_down"][P:I, :]).then_inc(w_loaded[2], 16)
            sp.dma_start(g["block_rows"][:], g["c_block_rows"]).then_inc(loaded, 16)
            sp.dma_start(g["head_mean"][:], g["c_head_mean"]).then_inc(loaded, 16)
            sp.dma_start(g["swap"][:], g["c_swap"]).then_inc(loaded, 16)
            sp.dma_start(g["rank"][:], g["c_rank"]).then_inc(loaded, 16)
            sp.wait_ge(consts, 16 * 16)

        @block.gpsimd
        def _(pool):
            for i in range(BUFS):
                pool.memset(g["q_head"][i][:], 0.0)
                pool.memset(g["k_head"][i][:], 1.0)

        @block.scalar
        def _(act):
            n = NT // 4
            for i in range(4):
                act.dma_start(g["x"][:, i * n:(i + 1) * n, :],
                              g["x_dram"][:, i * n:(i + 1) * n, :]).then_inc(x_loaded[i], 16)

        @block.tensor
        def _(pe):
            pe.wait_ge(consts, 16 * 16)
            for i in range(4):
                pe.transpose(ps[:, i, 0:D], raw[:, i, :], ident[:]).then_inc(turned, 1)
            pe.transpose(ps[:, 4, 0:E + 1], raw_gate[:], ident[0:E + 1, 0:E + 1]).then_inc(turned, 1)
            pe.matmul(ps[:, 5, 0:2], dim_rows[:], raw_nw[:], start=True, stop=True).then_inc(turned, 1)
            for i in range(2):
                for n in range(TPB):
                    last = pe.transpose(ps[0:HD // 2, 6 + i, n * P:(n + 1) * P], raw_rope[:, i, n, :], ident[:])
                last.then_inc(turned, 1)
            pe.wait_ge(lows, 4)
            for i in range(2):
                pe.wait_ge(copied, 7 + i)
                pe.matmul(ps[:, i, :], pair_rows[:, i, :], ropeT[:, i, :], start=True, stop=True).then_inc(turned, 1)

        @block.vector
        def _(dve):
            dve.memset(raw_w[0][:, R:], 0.0)
            dve.memset(raw_w[1][:, R:], 0.0)
            dve.memset(raw_w[2][32:64, (CH - 1) * P:], 0.0)
            dve.memset(raw_w[2][64:P, (CH - 1) * P:], 0.0)
            for part in g["gateT"]:
                dve.memset(part[:].bitcast(F32), 0.0)
            dve.memset(raw_rope[:, 0, :, :], 1.0).then_inc(filled, 1)
            dve.memset(raw_rope[:, 1, :, :], 0.0).then_inc(filled, 1)
            for i in range(BUFS):
                dve.memset(g["vals"][i][:, :, HD:HD1], 1.0)
                dve.memset(g["vals"][i][:, :, HD1:32], 0.0)
            for n in range(NT):
                if n % (NT // 4) == 0:
                    dve.wait_ge(x_loaded[n // (NT // 4)], 16)
                dve.bn_stats(g["stats"][:, n, :], g["x"][:, n, :])
            dve.wait_ge(turned, 6)
            small = [(g[w], ps[:, i, 0:D]) for i, w in enumerate(("wqT", "wkT", "wvT"))]
            small.append((g["gateT"], ps[:, 4, 0:E + 1]))
            for parts, made in small:
                dve.tensor_copy(parts[HI][:, 0:made.shape[-1]], made).then_inc(copied, 1)
            dve.tensor_copy(g["woT"][:], ps[:, 3, 0:D]).then_inc(copied, 1)
            dve.tensor_scalar(g["norm_w"][:, 0:1], ps[:, 5, 0:1], float(HD) ** -0.5, None, ALU.mult).then_inc(copied, 1)
            for i in range(2):
                dve.wait_ge(turned, 7 + i)
                dve.tensor_copy(ropeT[:, i, :], ps[0:HD // 2, 6 + i, :]).then_inc(copied, 1)
            dve.wait_ge(copied, 4)
            for parts, made in small:
                n = made.shape[-1]
                dve.tensor_tensor(parts[LO][:, 0:n], made, parts[HI][:, 0:n].bitcast(F32), ALU.subtract).then_inc(lows, 1)
            dve.tensor_copy(g["norm_w"][:, 1:2], ps[:, 5, 1:2])
            dve.tensor_copy(g["identb"][:], ident[:])
            dve.tensor_copy(g["expert_rows"][:], rows32[:])
            for i in range(2):
                dve.wait_ge(turned, 9 + i)
                dve.tensor_copy(g["rope"][:, i, :], ps[:, i, :])


def norm_phase(nc, sem, tag, ps, x, stats, xnT, ident, gateT=None, logits=None,
               weights=(), late=None):
    step = sem(tag + "_step")
    rooted = sem(tag + "_rooted")
    w_rounded = sem(tag + "_w_rounded")
    normed = sem(tag + "_normed")
    turned = sem(tag + "_turned")
    rounded = sem(tag + "_rounded")
    rest = sem(tag + "_rest")
    scored = sem(tag + "_scored")
    scored_kept = sem(tag + "_scored_kept")
    back = sem(tag + "_back")
    kept = sem(tag + "_kept")
    TURNED, SCORED, BACK, BANKS = 0, 3, 5, 3
    NE = E + 1
    with ExitStack() as tmp:
        def tb(name, shape):
            return tmp.enter_context(nc.sbuf_tensor(f"{tag}_{name}", shape, F32))
        total = tb("total", [P, NT])
        diff = tb("diff", [P, NT])
        within = tb("within", [P, NT])
        mean = tb("mean", [P, NT])
        between = tb("between", [P, NT])
        spread = tb("spread", [P, NT])
        var = tb("var", [P, NT])
        std = tb("std", [P, NT])
        rstd = tb("rstd", [P, NT])
        xn = tb("xn", [P, 2, TPB, D])
        scoresT = tb("scoresT", [NE, 2, BLK])
        block = tmp.enter_context(nc.Block())

        @block.vector
        def _(dve):
            even, odd = stats[:, :, 0:3], stats[:, :, 3:6]
            dve.tensor_tensor(total[:], even[:, :, 1], odd[:, :, 1], ALU.add).then_inc(step, 1)
            dve.tensor_tensor(diff[:], even[:, :, 1], odd[:, :, 1], ALU.subtract).then_inc(step, 1)
            dve.tensor_tensor(within[:], even[:, :, 2], odd[:, :, 2], ALU.add).then_inc(step, 1)
            dve.wait_ge(step, 3)
            dve.scalar_tensor_tensor(between[:], diff[:], 0.25, diff[:], ALU.mult, ALU.mult).then_inc(step, 1)
            dve.tensor_scalar(spread[:], within[:], 1.0 / D, LN_EPS, ALU.mult, ALU.add).then_inc(step, 1)
            dve.tensor_scalar(mean[:], total[:], 0.5, None, ALU.mult).then_inc(step, 1)
            dve.wait_ge(step, 6)
            dve.tensor_tensor(var[:], between[:], spread[:], ALU.add).then_inc(step, 1)
            dve.wait_ge(rooted, 1)
            dve.reciprocal(rstd[:], std[:]).then_inc(step, 1)
            dve.wait_ge(step, 8)

            def low(b):
                dve.wait_ge(rounded, b + 1)
                cols = slice(b * BLK, (b + 1) * BLK)
                dve.tensor_tensor(xnT[LO][:, cols], ps[:, TURNED + b % BANKS, :], xnT[HI][:, cols].bitcast(F32),
                                  ALU.subtract).then_inc(rest, 1)

            for b in range(NB):
                if b >= 2:
                    dve.wait_ge(turned, b - 1)
                for j in range(TPB):
                    n = b * TPB + j
                    last = dve.tensor_scalar(xn[:, b % 2, j, :], x[:, n, :], mean[:, n:n + 1], rstd[:, n:n + 1],
                                             ALU.subtract, ALU.mult)
                last.then_inc(normed, 1)
                if b >= 1:
                    low(b - 1)
            low(NB - 1)

        @block.tensor
        def _(pe):
            def route(b):
                pe.wait_ge(rest, b + 1)
                if b >= 2:
                    pe.wait_ge(scored_kept, b - 1)
                for n, (wp, xp) in enumerate(PASSES):
                    last = pe.matmul(ps[:, SCORED + b % 2, :], gateT[wp][:], xnT[xp][:, b * BLK:(b + 1) * BLK],
                                     start=(n == 0), stop=(n == len(PASSES) - 1))
                last.then_inc(scored, 1)

            def turn_back(b):
                pe.wait_ge(scored_kept, b + 1)
                if b >= 2:
                    pe.wait_ge(kept, b - 1)
                for j in range(TPB):
                    last = pe.transpose(ps[:, BACK + b % 2, j * NE:(j + 1) * NE], scoresT[:, b % 2, j * P:(j + 1) * P],
                                        ident[0:NE, 0:NE])
                last.then_inc(back, 1)

            for b in range(NB + 4):
                if b < NB:
                    pe.wait_ge(normed, b + 1)
                    if b >= BANKS:
                        pe.wait_ge(rest, b - BANKS + 1)
                    for j in range(TPB):
                        last = pe.transpose(ps[:, TURNED + b % BANKS, j * P:(j + 1) * P], xn[:, b % 2, j, :], ident[:])
                    last.then_inc(turned, 1)
                if gateT is not None and 2 <= b < NB + 2:
                    route(b - 2)
                if gateT is not None and b >= 4:
                    turn_back(b - 4)

        @block.scalar
        def _(act):
            act.wait_ge(step, 7)
            act.activation(std[:], var[:], ACT.Sqrt).then_inc(rooted, 1)
            for b in range(NB + 4):
                if b < NB:
                    act.wait_ge(turned, b + 1)
                    act.activation(xnT[HI][:, b * BLK:(b + 1) * BLK], ps[:, TURNED + b % BANKS, :], ACT.Copy).then_inc(rounded, 1)
                if gateT is not None and 2 <= b < NB + 2:
                    n = b - 2
                    act.wait_ge(scored, n + 1)
                    if n >= 2:
                        act.wait_ge(back, n - 1)
                    act.activation(scoresT[:, n % 2, :], ps[0:NE, SCORED + n % 2, :], ACT.Copy).then_inc(scored_kept, 1)
                if 1 <= b < 1 + len(weights):
                    raw, parts, arrived, dmas = weights[b - 1]
                    act.wait_ge(arrived, 16 * dmas)
                    act.activation(flat(parts[HI]), raw[:], ACT.Copy).then_inc(w_rounded, 1)
                if gateT is not None and b >= 4:
                    n = b - 4
                    act.wait_ge(back, n + 1)
                    act.activation(logits[:, n * TPB:(n + 1) * TPB, :],
                                   ps[:, BACK + n % 2, 0:TPB * NE].rearrange("p (n e) -> p n e", e=NE),
                                   ACT.Copy).then_inc(kept, 1)

        @block.gpsimd
        def _(pool):
            for i, (raw, parts, _, _) in enumerate(weights):
                pool.wait_ge(w_rounded, i + 1)
                pool.tensor_tensor(flat(parts[LO]), raw[:], flat(parts[HI]).bitcast(F32), ALU.subtract)

        if late is not None:
            @block.sync
            def _(sp):
                sp.wait_ge(*late)


def routing_phase(nc, sem, tag, ps, logits, rank, identb, combT):
    step = sem(tag + "_step")
    shifted = sem(tag + "_shifted")
    exped = sem(tag + "_exped")
    split = sem(tag + "_split")
    turned = sem(tag + "_turned")
    kept = [sem(f"{tag}_kept{i}") for i in range(2)]
    NE = E + 1
    BANKS = 4
    with ExitStack() as tmp:
        def tb(name, shape, dt=F32):
            return tmp.enter_context(nc.sbuf_tensor(f"{tag}_{name}", shape, dt))
        ex = tb("ex", [P, NT, E])
        ex9 = tb("ex9", [P, NT, 1])
        prob = tb("prob", [P, NT, E])
        key = tb("key", [P, NT, E])
        first = tb("first", [P, NT, E])
        both = tb("both", [P, NT, E])
        rest = tb("rest", [P, NT, E])
        top = tb("top", [P, 6, NT])
        comb = tb("comb", [P, NT, NE])
        resid = tb("resid", [P, NT, NE])
        parts = tb("parts", [P, NT, 3, NE], BF16)
        block = tmp.enter_context(nc.Block())

        def wide(a):
            return a.unsqueeze(2).broadcast_to([P, NT, E])

        @block.vector
        def _(dve):
            count = [0]

            def then(ins):
                count[0] += 1
                ins.then_inc(step, 1)
                dve.wait_ge(step, count[0])

            lg = logits[:, :, 0:E]
            then(dve.tensor_reduce(top[:, 0, :], lg, AX.X, ALU.max))
            dve.tensor_tensor(ex[:], lg, wide(top[:, 0, :]), ALU.subtract).then_inc(shifted, 1)
            dve.wait_ge(exped, 2)
            then(dve.tensor_reduce(top[:, 1, :], ex[:], AX.X, ALU.add))
            then(dve.reciprocal(top[:, 2, :], top[:, 1, :]))
            then(dve.tensor_tensor(prob[:], ex[:], wide(top[:, 2, :]), ALU.mult))
            then(dve.tensor_reduce(top[:, 0, :], prob[:], AX.X, ALU.max))
            then(dve.tensor_tensor(key[:], prob[:], wide(top[:, 0, :]), ALU.is_equal))
            then(dve.tensor_tensor(key[:], key[:], rank[:].unsqueeze(1).broadcast_to([P, NT, E]), ALU.mult))
            then(dve.tensor_reduce(top[:, 3, :], key[:], AX.X, ALU.max))
            then(dve.tensor_tensor(first[:], key[:], wide(top[:, 3, :]), ALU.is_equal))
            then(dve.scalar_tensor_tensor(rest[:], first[:], -2.0, prob[:], ALU.mult, ALU.add))
            then(dve.tensor_reduce(top[:, 1, :], rest[:], AX.X, ALU.max))
            then(dve.tensor_tensor(key[:], rest[:], wide(top[:, 1, :]), ALU.is_equal))
            then(dve.tensor_tensor(key[:], key[:], rank[:].unsqueeze(1).broadcast_to([P, NT, E]), ALU.mult))
            then(dve.tensor_reduce(top[:, 3, :], key[:], AX.X, ALU.max))
            then(dve.tensor_tensor(both[:], key[:], wide(top[:, 3, :]), ALU.is_equal))
            then(dve.tensor_tensor(both[:], both[:], first[:], ALU.add))
            then(dve.tensor_tensor(top[:, 4, :], top[:, 0, :], top[:, 1, :], ALU.add))
            then(dve.reciprocal(top[:, 5, :], top[:, 4, :]))
            then(dve.tensor_tensor(both[:], both[:], prob[:], ALU.mult))
            then(dve.tensor_tensor(comb[:, :, 0:E], both[:], wide(top[:, 5, :]), ALU.mult))
            then(dve.tensor_scalar(ex9[:], ex9[:], 1.0, None, ALU.add))
            then(dve.reciprocal(comb[:, :, E:NE], ex9[:]))
            then(dve.tensor_copy(parts[:, :, 0, :], comb[:]))
            then(dve.tensor_tensor(resid[:], comb[:], parts[:, :, 0, :], ALU.subtract))
            then(dve.tensor_copy(parts[:, :, 1, :], resid[:]))
            dve.tensor_tensor(parts[:, :, 2, :], resid[:], parts[:, :, 1, :], ALU.subtract).then_inc(split, 1)
            for b in range(1, NB, 2):
                dve.wait_ge(turned, b + 1)
                dve.tensor_copy(combT[:, b * BLK:(b + 1) * BLK],
                                ps[0:3 * NE, b % BANKS, :].bitcast(BF16)[:, 0:BLK]).then_inc(kept[1], 1)

        @block.scalar
        def _(act):
            act.activation(ex9[:], logits[:, :, E:NE], ACT.Exp, scale=-1.0).then_inc(exped, 1)
            act.wait_ge(shifted, 1)
            act.activation(ex[:], ex[:], ACT.Exp).then_inc(exped, 1)
            for b in range(0, NB, 2):
                act.wait_ge(turned, b + 1)
                act.activation(combT[:, b * BLK:(b + 1) * BLK],
                               ps[0:3 * NE, b % BANKS, :].bitcast(BF16)[:, 0:BLK], ACT.Copy).then_inc(kept[0], 1)

        @block.tensor
        def _(pe):
            pe.wait_ge(split, 1)
            for b in range(NB):
                if b >= BANKS:
                    pe.wait_ge(kept[b % 2], (b - BANKS) // 2 + 1)
                for j in range(TPB):
                    last = pe.transpose(ps[0:3 * NE, b % BANKS, :].bitcast(BF16)[:, j * P:(j + 1) * P],
                                        parts[:, b * TPB + j, :, :].rearrange("p a e -> p (a e)"), identb[:])
                last.then_inc(turned, 1)


def expert_phase(nc, sem, tag, ps, x, xnT, wgate, wup, wdown, expert_rows, combT, ident, stats=None,
                 out_dram=None):
    gated = sem(tag + "_gated")
    upped = sem(tag + "_upped")
    spread = sem(tag + "_spread")
    silued = sem(tag + "_silued")
    product = sem(tag + "_product")
    weighted = sem(tag + "_weighted")
    rounded = sem(tag + "_rounded")
    hidden_ready = sem(tag + "_hidden_ready")
    summed = sem(tag + "_summed")
    summed_kept = sem(tag + "_summed_kept")
    turned = sem(tag + "_turned")
    added = sem(tag + "_added")
    stored = sem(tag + "_stored")
    rows = [P] * (CH - 1) + [TAIL]
    SLOTS = 4
    fours = 2 * CH - 3 * (-2 * CH % SLOTS)
    slot = [n % SLOTS if n < fours else (n - fours) % 3 for n in range(2 * CH)]
    assert fours >= 0 and fours % SLOTS == 0
    with ExitStack() as tmp:
        def tb(name, shape, dt=F32):
            return tmp.enter_context(nc.sbuf_tensor(f"{tag}_{name}", shape, dt))
        silu = tb("silu", [P, 2, BLK])
        prod = tb("prod", [P, 2, BLK])
        full = tb("full", [P, 2, BLK])
        hidden = [tb("hidden" + part, [P, SLOTS, BLK], F32R) for part in ("_hi", "_lo")]
        yT = tb("yT", [P, BLK])
        block = tmp.enter_context(nc.Block())
        GATE, UP, SPREAD, Y, YT = 0, 2, 4, 6, 7

        def over_blocks(eng, first, turn):
            first()
            with eng.Fori(0, NB // 2 - 1) as it:
                for par in range(2):
                    turn(it * 2 + par, par, False)
            turn(NB - 2, 0, False)
            turn(NB - 1, 1, True)

        @block.tensor
        def _(pe):
            def up(blk, par, c):
                n, i, cols = blk * CH + c, (par + c) % 2, slice(c * P, (c + 1) * P)
                tokens = bass.ds(blk * BLK, BLK)
                if not (isinstance(n, int) and n < 2):
                    pe.wait_ge(weighted, n - 1)
                for bank, w, done in ((GATE, wgate, gated), (UP, wup, upped))[:1 if c == CH - 1 else 2]:
                    for m, (wp, xp) in enumerate(PASSES):
                        last = pe.matmul(ps[:, bank + i, :], w[wp][:, cols], xnT[xp][:, tokens],
                                         start=(m == 0), stop=(m == len(PASSES) - 1))
                    last.then_inc(done, 1)
                pe.matmul(ps[:, SPREAD + i, :], expert_rows[:, cols], combT[:, tokens],
                          start=True, stop=True).then_inc(spread, 1)

            def down(blk, par, c):
                pe.wait_ge(hidden_ready, blk * CH + c + 1)
                if c == 0:
                    pe.wait_ge(summed_kept, blk + PRIME)
                at = slot[par * CH + c]
                for m, (wp, hp) in enumerate(PASSES):
                    last = pe.matmul(ps[:, Y, :], wdown[wp][0:rows[c], c, :], hidden[hp][0:rows[c], at, :],
                                     start=(c == 0 and m == 0), stop=(c == CH - 1 and m == len(PASSES) - 1))
                if c == CH - 1:
                    last.then_inc(summed, 1)

            def first():
                for c in range(3):
                    up(0, 0, c)
                down(0, 0, 0)

            def turn(blk, par, last):
                for c in range(3, CH + 3):
                    if c < CH:
                        up(blk, par, c)
                    elif not last:
                        up(blk + 1, 1 - par, c - CH)
                    if c - 2 < CH:
                        down(blk, par, c - 2)
                    elif not last:
                        down(blk + 1, 1 - par, c - 2 - CH)
                pe.wait_ge(summed_kept, blk + 1 + PRIME)
                pe.wait_ge(added, blk + PRIME)
                for j in range(TPB):
                    tr = pe.transpose(ps[:, YT, j * P:(j + 1) * P], yT[:, j * P:(j + 1) * P], ident[:])
                tr.then_inc(turned, 1)

            over_blocks(pe, first, turn)

        @block.scalar
        def _(act):
            def gate(blk, par, c):
                i = (par + c) % 2
                act.wait_ge(gated, blk * CH + c + 1)
                act.activation(silu[0:rows[c], i, :], ps[0:rows[c], GATE + i, :], ACT.Silu).then_inc(silued, 1)

            def round_hidden(blk, par, c):
                act.wait_ge(weighted, blk * CH + c + 1)
                act.activation(hidden[HI][0:rows[c], slot[par * CH + c], :], full[0:rows[c], (par + c) % 2, :],
                               ACT.Copy).then_inc(rounded, 1)

            def first():
                gate(0, 0, 0)
                gate(0, 0, 1)
                round_hidden(0, 0, 0)

            def turn(blk, par, last):
                for c in range(1, CH + 1):
                    if c + 1 < CH:
                        gate(blk, par, c + 1)
                    elif not last:
                        gate(blk + 1, 1 - par, c + 1 - CH)
                    if c < CH:
                        round_hidden(blk, par, c)
                    elif not last:
                        round_hidden(blk + 1, 1 - par, 0)
                act.wait_ge(summed, blk + 1)
                act.activation(yT[:], ps[:, Y, :], ACT.Copy).then_inc(summed_kept, 1)

            prime(act, summed_kept)
            over_blocks(act, first, turn)

        @block.vector
        def _(dve):
            def weigh(blk, par, c):
                n, i = blk * CH + c, (par + c) % 2
                dve.wait_ge(silued, n + 1)
                up = ps[TAIL_UP:TAIL_UP + TAIL, GATE + i, :]
                if c < CH - 1:
                    dve.wait_ge(upped, blk * (CH - 1) + c + 1)
                    up = ps[:, UP + i, :]
                dve.tensor_tensor(prod[0:rows[c], i, :], silu[0:rows[c], i, :], up, ALU.mult).then_inc(product, 1)
                dve.wait_ge(product, n + 1)
                dve.wait_ge(spread, n + 1)
                if not (isinstance(n, int) and n < 2):
                    dve.wait_ge(hidden_ready, n - 1)
                dve.tensor_tensor(full[0:rows[c], i, :], prod[0:rows[c], i, :], ps[0:rows[c], SPREAD + i, :],
                                  ALU.mult).then_inc(weighted, 1)

            def first():
                for c in range(3 + TPB):
                    weigh(0, 0, c)

            def turn(blk, par, last):
                for c in range(3 + TPB, CH + 3):
                    if c < CH:
                        weigh(blk, par, c)
                    elif not last:
                        weigh(blk + 1, 1 - par, c - CH)
                dve.wait_ge(turned, blk + 1)
                tiles = x[:, bass.ds(blk * TPB, TPB), :].rearrange("p n d -> p (n d)")
                dve.scalar_tensor_tensor(tiles, ps[:, YT, :], 0.5, tiles, ALU.mult, ALU.add).then_inc(added, 1)
                for j in range(TPB):
                    if not last:
                        weigh(blk + 1, 1 - par, 3 + j)
                    if stats is not None:
                        dve.wait_ge(added, blk + 1 + PRIME)
                        dve.bn_stats(stats[:, bass.ds(blk * TPB + j, 1), :].rearrange("p n s -> p (n s)"),
                                     x[:, bass.ds(blk * TPB + j, 1), :].rearrange("p n d -> p (n d)"))

            prime(dve, added)
            over_blocks(dve, first, turn)

        @block.gpsimd
        def _(pool):
            with pool.Fori(0, NB // 2) as it:
                for n2 in range(2 * CH):
                    pool.wait_ge(rounded, it * 2 * CH + n2 + 1)
                    r = rows[n2 % CH]
                    pool.tensor_tensor(hidden[LO][0:r, slot[n2], :], full[0:r, n2 % 2, :],
                                       hidden[HI][0:r, slot[n2], :].bitcast(F32), ALU.subtract).then_inc(hidden_ready, 1)

        if out_dram is not None:
            @block.sync
            def _(sp):
                with sp.Fori(0, NB) as blk:
                    sp.wait_ge(added, blk + 1 + PRIME)
                    sp.dma_start(out_dram[:, bass.ds(blk * TPB, TPB), :],
                                 x[:, bass.ds(blk * TPB, TPB), :]).then_inc(stored, 16)
                sp.wait_ge(stored, 16 * NB)


def qkv_phase(nc, sem, ps, xnT, weights, norm_w, head_mean, swap, rope, ident, v, q_rows, k_rows,
              q_head, k_head, qk_loaded, stored):
    projected = sem("qk_projected")
    v_projected = sem("qk_v_projected")
    v_kept = sem("qk_v_kept")
    squared = sem("qk_squared")
    meaned = sem("qk_meaned")
    eps_set = sem("qk_eps_set")
    rooted = sem("qk_rooted")
    inverted = sem("qk_inverted")
    widened = sem("qk_widened")
    spread = sem("qk_spread")
    spread_kept = sem("qk_spread_kept")
    normed = sem("qk_normed")
    swapped = sem("qk_swapped")
    cosed = sem("qk_cosed")
    sined = sem("qk_sined")
    roped = sem("qk_roped")
    part0 = sem("qk_part0")
    rest1 = sem("qk_rest1")
    part1 = sem("qk_part1")
    part2 = sem("qk_part2")
    turned_blocks = [b * BPS + BPS - 1 for b in range(BATCH)]
    ORDER = turned_blocks + [n for n in range(NB) if n not in turned_blocks]
    FIRST_DONE = max(ORDER.index(n) for n in range(BPS))
    assert FIRST_DONE + BUFS <= NB
    assert len(turned_blocks) <= 2
    QK, V, MEAN = 0, 4, 6
    BACK = (7, 5)
    SWAP = BACK[1]
    FACTORS = 2 * TPB * HEADS
    with ExitStack() as tmp:
        def tb(name, shape, dt=F32):
            return tmp.enter_context(nc.sbuf_tensor("qk_" + name, shape, dt))
        eps = tb("eps", [P, 1])
        sq = tb("sq", [P, 2, 2, BLK])
        root = tb("root", [P, FACTORS])
        inv = tb("inv", [P, FACTORS])
        rstd = tb("rstd", [P, 2, 2, BLK])
        qn = tb("qn", [P, 2, 2, BLK])
        left = tb("left", [P, 2, 2, BLK])
        parts = tb("parts", [P, 2, 2, 3, BLK], BF16)
        block = tmp.enter_context(nc.Block())

        @block.tensor
        def _(pe):
            def project(m):
                cols = ORDER[m] * BLK
                for i in range(2):
                    if m >= 2:
                        pe.wait_ge(normed, 2 * (m - 2) + i + 1)
                    for n, (wp, xp) in enumerate(PASSES):
                        last = pe.matmul(ps[:, QK + 2 * (m % 2) + i, :], weights[i][wp][:], xnT[xp][:, cols:cols + BLK],
                                         start=(n == 0), stop=(n == len(PASSES) - 1))
                    last.then_inc(projected, 1)

            def project_v(m):
                if m >= 1:
                    pe.wait_ge(v_kept, m)
                for j in range(TPB):
                    tokens = slice(ORDER[m] * BLK + j * P, ORDER[m] * BLK + (j + 1) * P)
                    for n, (xp, wp) in enumerate(PASSES):
                        last = pe.matmul(ps[:, V, j * D:(j + 1) * D], xnT[xp][:, tokens], weights[2][wp][:],
                                         start=(n == 0), stop=(n == len(PASSES) - 1))
                last.then_inc(v_projected, 1)

            def mean(m):
                if m >= 1:
                    pe.wait_ge(rooted, m)
                for i in range(2):
                    pe.wait_ge(squared, 2 * m + i + 1)
                    for j in range(TPB):
                        at = (i * TPB + j) * HEADS
                        last = pe.matmul(ps[:, MEAN, at:at + HEADS], sq[:, m % 2, i, j * P:(j + 1) * P], head_mean[:],
                                         start=True, stop=True)
                last.then_inc(meaned, 1)

            def spread_back(m, i):
                pe.wait_ge(widened, 2 * m + i + 1)
                if m >= 1:
                    pe.wait_ge(spread_kept, 2 * (m - 1) + i + 1)
                    if m - 1 < len(turned_blocks) and BACK[i] == SWAP:
                        pe.wait_ge(sined, 2 * m)
                for j in range(TPB):
                    last = pe.transpose(ps[:, BACK[i], j * P:(j + 1) * P], rstd[:, m % 2, i, j * P:(j + 1) * P], ident[:])
                last.then_inc(spread, 1)

            def exchange(m):
                for i in range(2):
                    pe.wait_ge(normed, 2 * m + i + 1)
                    pe.wait_ge(spread_kept, 2 * m + 2)
                    if i:
                        pe.wait_ge(sined, 2 * m + 1)
                    pe.matmul(ps[:, SWAP, :], swap[:], qn[:, m % 2, i, :], start=True, stop=True).then_inc(swapped, 1)

            project(0)
            project_v(0)
            for m in range(NB):
                mean(m)
                if m < NB - 1:
                    project(m + 1)
                spread_back(m, 0)
                spread_back(m, 1)
                if m < NB - 1:
                    project_v(m + 1)
                if m < len(turned_blocks):
                    exchange(m)

        @block.scalar
        def _(act):
            def square(m, i):
                act.wait_ge(projected, 2 * m + i + 1)
                act.activation(sq[:, m % 2, i, :], ps[:, QK + 2 * (m % 2) + i, :], ACT.Square).then_inc(squared, 1)

            def keep_v(m):
                act.wait_ge(v_projected, m + 1)
                b, n = divmod(ORDER[m], BPS)
                act.activation(v[:, b, :, n * TPB:(n + 1) * TPB, :].rearrange("p h t d -> p t h d"),
                               ps[:, V, :].rearrange("p (t h d) -> p t h d", t=TPB, h=HEADS),
                               ACT.Copy).then_inc(v_kept, 1)

            act.wait_ge(eps_set, 1)
            square(0, 0)
            square(0, 1)
            keep_v(0)
            for m in range(NB):
                act.wait_ge(meaned, m + 1)
                if m >= 1:
                    act.wait_ge(inverted, m)
                act.activation(root[:], ps[:, MEAN, 0:FACTORS], ACT.Sqrt, bias=eps[:]).then_inc(rooted, 1)
                if m < NB - 1:
                    square(m + 1, 0)
                act.wait_ge(inverted, m + 1)
                for i in range(2):
                    act.activation(rstd[:, m % 2, i, :].rearrange("p (n d) -> p n d", d=HD),
                                   inv[:, i * TPB * HEADS:(i + 1) * TPB * HEADS].unsqueeze(2).broadcast_to([P, TPB * HEADS, HD]),
                                   ACT.Copy).then_inc(widened, 1)
                if m < NB - 1:
                    square(m + 1, 1)
                for i in range(2):
                    act.wait_ge(spread, 2 * m + i + 1)
                    act.activation(rstd[:, m % 2, i, :], ps[:, BACK[i], :], ACT.Copy).then_inc(spread_kept, 1)
                if m < NB - 1:
                    keep_v(m + 1)
                for i in range(2):
                    act.wait_ge(roped if m < len(turned_blocks) else normed, 2 * m + i + 1)
                    if m >= 2:
                        act.wait_ge(stored[m % 2], 16 * 2 * (m // 2))
                    act.activation(parts[:, m % 2, i, 0, :], qn[:, m % 2, i, :], ACT.Copy).then_inc(part0, 1)

        @block.vector
        def _(dve):
            def split(m):
                par = m % 2
                for i in range(2):
                    dve.wait_ge(part0, 2 * m + i + 1)
                    dve.tensor_tensor(left[:, par, i, :], qn[:, par, i, :], parts[:, par, i, 0, :],
                                      ALU.subtract).then_inc(rest1, 1)
                for i in range(2):
                    dve.wait_ge(rest1, 2 * m + i + 1)
                    dve.tensor_copy(parts[:, par, i, 1, :], left[:, par, i, :]).then_inc(part1, 1)

            dve.memset(eps[:], RMS_EPS).then_inc(eps_set, 1)
            for m in range(NB):
                par = m % 2
                dve.wait_ge(rooted, m + 1)
                if m >= 1:
                    dve.wait_ge(widened, 2 * m)
                dve.reciprocal(inv[:], root[:]).then_inc(inverted, 1)
                if m >= 1:
                    split(m - 1)
                for i in range(2):
                    dve.wait_ge(spread_kept, 2 * m + i + 1)
                    dve.scalar_tensor_tensor(qn[:, par, i, :], ps[:, QK + 2 * par + i, :], norm_w[:, i:i + 1],
                                             rstd[:, par, i, :], ALU.mult, ALU.mult).then_inc(normed, 1)
                if m < len(turned_blocks):
                    for i in range(2):
                        dve.wait_ge(normed, 2 * m + i + 1)
                        dve.tensor_tensor(left[:, par, i, :], qn[:, par, i, :], rope[:, 0, :], ALU.mult).then_inc(cosed, 1)
                    for i in range(2):
                        dve.wait_ge(swapped, 2 * m + i + 1)
                        dve.tensor_tensor(rstd[:, par, i, :], ps[:, SWAP, :], rope[:, 1, :], ALU.mult).then_inc(sined, 1)
                    for i in range(2):
                        dve.wait_ge(cosed, 2 * m + i + 1)
                        dve.wait_ge(sined, 2 * m + i + 1)
                        dve.tensor_tensor(qn[:, par, i, :], left[:, par, i, :], rstd[:, par, i, :],
                                          ALU.add).then_inc(roped, 1)
            split(NB - 1)

        @block.gpsimd
        def _(pool):
            for m in range(NB):
                for i in range(2):
                    pool.wait_ge(part1, 2 * m + i + 1)
                    pool.tensor_tensor(parts[:, m % 2, i, 2, :], left[:, m % 2, i, :], parts[:, m % 2, i, 1, :],
                                       ALU.subtract).then_inc(part2, 1)

        @block.sync
        def _(sp):
            for m in range(NB):
                b, n = divmod(ORDER[m], BPS)
                for i, rows in enumerate((q_rows, k_rows)):
                    sp.wait_ge(part2, 2 * m + i + 1)
                    heads = rows[b * HEADS:(b + 1) * HEADS, :, :, n * BLK:(n + 1) * BLK]
                    sp.dma_start(heads.rearrange("h d j t -> (h d) j t"), parts[:, m % 2, i, :, :]).then_inc(stored[m % 2], 16)
                if m == FIRST_DONE:
                    for i in range(2):
                        sp.wait_ge(stored[i], 16 * 2 * len(range(i, m + 1, 2)))
                h = m - FIRST_DONE
                if 0 <= h < BUFS:
                    load_head(sp, q_head[h], k_head[h], q_rows[h], k_rows[h], qk_loaded[h])


LOAD_DMAS = 6
assert PAIRS == [(a, b) for a in range(3) for b in range(3 - a)]


def load_head(sp, q, k, q_rows, k_rows, loaded):
    for part in range(3):
        first = PAIRS.index((part, 0))
        times = 3 - part
        rows = slice(first * HD, (first + times) * HD)
        same = q_rows[:, part, :].unsqueeze(0).broadcast_to([times, HD, SEQ])
        sp.dma_start(q[rows, :], same).then_inc(loaded, 16)
        sp.dma_start(k[rows, :], k_rows[:, 0:times, :].rearrange("d j t -> j d t")).then_inc(loaded, 16)


SUM_DMAS = BPS
ROWS_OF_BATCH = HEADS * BPS


def load_sums(sp, b, sum_rows, o, den, loaded):
    heads = sum_rows[b * HEADS:(b + 1) * HEADS]
    sp.dma_start(den[b * ROWS_OF_BATCH:(b + 1) * ROWS_OF_BATCH, :],
                 heads[:, HD, :].rearrange("h (n t) -> h n t", n=BPS)).then_inc(loaded, 16)
    for n in range(BPS):
        sp.dma_start(o[:, n, :], heads[:, 0:HD, n * BLK:(n + 1) * BLK]).then_inc(loaded, 16)


def attention_phase(nc, sem, kept, ps, v, identb, q, k, vals, q_rows, k_rows, qk_loaded, qk_stored,
                    sum_rows, sums_stored, o_loaded, inverted):
    CHUNKS = SEQ // BLK
    STEPS = KT * CHUNKS
    AHEAD, LAG = 2, 9
    TURNS = BH - AHEAD
    assert TURNS % BUFS == 0 and STEPS % BUFS == 1
    max_scored = sem("at_max_scored")
    max_reduced = sem("at_max_reduced")
    max_step = sem("at_max_step")
    max_turned = sem("at_max_turned")
    max_kept = sem("at_max_kept")
    max_placed = sem("at_max_placed")
    scored = sem("at_scored")
    exped = sem("at_exped")
    weighed = sem("at_weighed")
    values_placed = sem("at_values_placed")
    sums_kept = sem("at_sums_kept")
    VSTEPS = 5
    BETWEEN = 2
    TURN_MAXIMA = LAG + 3
    with ExitStack() as tmp:
        mx = kept("mx", [P, KT, CHUNKS])
        neg = kept("neg", [P, KT])
        res = kept("res", [P, KT])
        mparts = kept("mparts", [P, MR, KT], BF16)
        mrows = kept("mrows", [MR * KT, P], BF16)
        sums = kept("sums", [P, BLK])
        o = kept("o", [P, BPS, BLK])
        den = kept("den", [P, BLK])
        inv = kept("inv", [P, BLK])
        prob = tmp.enter_context(nc.sbuf_tensor("at_prob", [P, PROBS, CHUNKS, BLK], F32))
        block = tmp.enter_context(nc.Block())
        S, M, O, X = 0, 3, 6, 7

        @block.gpsimd
        def _(pool):
            def place(h, i):
                head = v[:].rearrange("p b h t d -> p (b h) t d")[:, h, :, :]
                pool.tensor_copy(vals[i][:, :, 0:HD], head).then_inc(values_placed, 1)

            for i in range(BUFS):
                place(i, i)

            def replace(h, i):
                pool.wait_ge(weighed, (h + 1) * KT + PRIME)
                place(h + BUFS, i)

            with pool.Fori(0, BH // BUFS - 1) as it:
                for i in range(BUFS):
                    replace(it * BUFS + i, i)
            for h in range((BH // BUFS - 1) * BUFS, BH - BUFS):
                replace(h, h % BUFS)

        @block.sync
        def _(sp):
            def place_maxima(h, i):
                sp.wait_ge(max_kept, h + 1)
                sp.dma_start(q[i][MROW:MROW + MR, :], mrows[:]).then_inc(max_placed, 16)

            def store_sums(h):
                sp.wait_ge(sums_kept, h + 1 + PRIME)
                for c in range(CHUNKS):
                    cols = slice(c * BLK, (c + 1) * BLK)
                    sp.dma_start(sum_rows[h][:, cols], sums[32 * c:32 * c + HD1, :]).then_inc(sums_stored, 16)

            def turn(h, i):
                place_maxima(h + 1, (i + 1) % BUFS)
                sp.wait_ge(weighed, (h + 1) * KT + PRIME)
                load_head(sp, q[i], k[i], q_rows[h + BUFS], k_rows[h + BUFS], qk_loaded[i])
                store_sums(h)

            prime(sp, sums_stored)
            for i in range(2):
                sp.wait_ge(qk_stored[i], 16 * NB)
            place_maxima(0, 0)
            with sp.Fori(0, BH // BUFS - 1) as it:
                for i in range(BUFS):
                    turn(it * BUFS + i, i)
            for h in range((BH // BUFS - 1) * BUFS, BH):
                if h < BH - BUFS:
                    turn(h, h % BUFS)
                else:
                    if h < BH - 1:
                        place_maxima(h + 1, (h + 1) % BUFS)
                    store_sums(h)
                if h == BH - 2:
                    load_sums(sp, 0, sum_rows, o, den, o_loaded[0])

        @block.scalar
        def _(act):
            def exps(h, i, g):
                for c in range(CHUNKS):
                    n = h * STEPS + g * CHUNKS + c
                    act.wait_ge(scored, n + 1)
                    act.activation(prob[:, g % PROBS, c, :], ps[:, S + (i + g * CHUNKS + c) % BUFS, :],
                                   ACT.Exp).then_inc(exped, 1)

            def keep_sums(h):
                act.wait_ge(weighed, (h + 1) * KT + PRIME)
                act.wait_ge(sums_stored, 16 * SUM_DMAS * h + PRIME)
                act.activation(sums[:], ps[:, O, :], ACT.Copy).then_inc(sums_kept, 1)

            def keep_maxima(h):
                act.wait_ge(max_turned, h + 1 + PRIME)
                if not (isinstance(h, int) and h == 0):
                    act.wait_ge(max_placed, 16 * h)
                act.activation(mrows[:], ps[0:MR * KT, X, 0:P], ACT.Copy).then_inc(max_kept, 1)

            def turn(h, i, last=False):
                for g in range(1, KT):
                    if not (isinstance(h, int) and h == 0 and g < PROBS):
                        act.wait_ge(weighed, h * KT + max(g - PROBS, -1) + 1 + PRIME)
                    exps(h, i, g)
                    if g == TURN_MAXIMA + 1 and not last:
                        keep_maxima(h + 1)
                if not last:
                    act.wait_ge(weighed, (h + 1) * KT - PROBS + 1 + PRIME)
                    exps(h + 1, i + 1, 0)
                keep_sums(h)

            prime(act, sums_kept)
            keep_maxima(0)
            exps(0, 0, 0)
            with act.Fori(0, TURNS // BUFS) as it:
                for i in range(BUFS):
                    turn(it * BUFS + i, i)
            turn(BH - 2, (BH - 2) % BUFS)
            turn(BH - 1, (BH - 1) % BUFS, last=True)

        @block.tensor
        def _(pe):
            def maxima(h, i, j):
                n, c = h * STEPS + j, j % CHUNKS
                if not (isinstance(n, int) and n < BUFS):
                    pe.wait_ge(max_reduced, n - BUFS + 1)
                pe.matmul(ps[:, M + (i + j) % BUFS, :], q[i][0:MROW, (j // CHUNKS) * P:(j // CHUNKS + 1) * P],
                          k[i][0:MROW, c * BLK:(c + 1) * BLK], start=True, stop=True).then_inc(max_scored, 1)

            def turn_maxima(h):
                pe.wait_ge(max_step, (h + 1) * VSTEPS)
                pe.matmul(ps[0:MR * KT, X, 0:P], mparts[:].rearrange("p a t -> p (a t)"), identb[:],
                          start=True, stop=True).then_inc(max_turned, 1)

            def scores(h, i, g, c):
                n = h * STEPS + g * CHUNKS + c
                if not (isinstance(n, int) and n < BUFS):
                    pe.wait_ge(exped, n - BUFS + 1)
                pe.matmul(ps[:, S + (i + g * CHUNKS + c) % BUFS, :], k[i][:, g * P:(g + 1) * P],
                          q[i][:, c * BLK:(c + 1) * BLK], start=True, stop=True).then_inc(scored, 1)

            def weigh(h, i, g):
                pe.wait_ge(exped, h * STEPS + (g + 1) * CHUNKS)
                if g == 0:
                    pe.wait_ge(values_placed, h + 1)
                    pe.wait_ge(sums_kept, h + PRIME)
                for c in range(CHUNKS):
                    last = pe.matmul(ps[32 * c:32 * c + 32, O, :], vals[i][:, g, :], prob[:, g % PROBS, c, :],
                                     start=(g == 0), stop=(g == KT - 1), skip_group_check=True)
                last.then_inc(weighed, 1)

            def turn(h, i, loads=None, last=False):
                nxt, far = (i + 1) % BUFS, (i + AHEAD) % BUFS
                for g in range(1, KT + 1):
                    if g == LAG + 1 and loads is not None:
                        pe.wait_ge(qk_loaded[far], 16 * LOAD_DMAS * loads)
                    if g == KT and not last:
                        pe.wait_ge(max_placed, 16 * (h + 2))
                    for c in range(CHUNKS):
                        if g < KT:
                            scores(h, i, g, c)
                        elif not last:
                            scores(h + 1, nxt, 0, c)
                        if g <= LAG and not last:
                            maxima(h + 1, nxt, (KT - LAG + g - 1) * CHUNKS + c)
                        elif g > LAG and loads is not None:
                            maxima(h + AHEAD, far, (g - LAG - 1) * CHUNKS + c)
                    weigh(h, i, g - 1)
                    if g == TURN_MAXIMA and not last:
                        turn_maxima(h + 1)

            prime(pe, weighed, max_turned)
            for h in range(AHEAD):
                pe.wait_ge(qk_loaded[h], 16 * LOAD_DMAS)
                for j in range(STEPS if h == 0 else (KT - LAG) * CHUNKS):
                    maxima(h, h, j)
                    if h == 1 and j == 3 * CHUNKS:
                        turn_maxima(0)
            pe.wait_ge(max_placed, 16)
            for c in range(CHUNKS):
                scores(0, 0, 0, c)
            with pe.Fori(0, TURNS // BUFS) as it:
                for i in range(BUFS):
                    turn(it * BUFS + i, i, loads=it + 1 + (i + AHEAD) // BUFS)
            turn(BH - 2, (BH - 2) % BUFS)
            turn(BH - 1, (BH - 1) % BUFS, last=True)

        @block.vector
        def _(dve):
            def reduce(h, i, j):
                dve.wait_ge(max_scored, h * STEPS + j + 1)
                dve.tensor_reduce(mx[:, j // CHUNKS, j % CHUNKS:j % CHUNKS + 1], ps[:, M + (i + j) % BUFS, :],
                                  AX.X, ALU.max).then_inc(max_reduced, 1)

            def turn(h, i, last=False):
                for j in range(BETWEEN * (VSTEPS - 1), STEPS):
                    reduce(h, i, j)
                at = h * VSTEPS
                dve.wait_ge(max_reduced, h * STEPS + STEPS)
                dve.tensor_reduce(neg[:], mx[:], AX.X, ALU.max, negate=True).then_inc(max_step, 1)
                dve.wait_ge(max_turned, h + PRIME)
                for step in range(1, VSTEPS):
                    dve.wait_ge(max_step, at + step)
                    if not last:
                        for j in range(BETWEEN * (step - 1), BETWEEN * step):
                            reduce(h + 1, (i + 1) % BUFS, j)
                    if step == 1:
                        dve.tensor_copy(mparts[:, 0, :], neg[:]).then_inc(max_step, 1)
                    elif step == 2:
                        dve.tensor_tensor(res[:], neg[:], mparts[:, 0, :], ALU.subtract).then_inc(max_step, 1)
                    elif step == 3:
                        dve.tensor_copy(mparts[:, 1, :], res[:]).then_inc(max_step, 1)
                    else:
                        dve.tensor_tensor(mparts[:, 2, :], res[:], mparts[:, 1, :], ALU.subtract).then_inc(max_step, 1)

            for j in range(BETWEEN * (VSTEPS - 1)):
                reduce(0, 0, j)
            with dve.Fori(0, TURNS // BUFS) as it:
                for i in range(BUFS):
                    turn(it * BUFS + i, i)
            for h in range(TURNS, BH):
                turn(h, h % BUFS, last=(h == BH - 1))
            dve.wait_ge(o_loaded[0], 16 * (1 + BPS))
            dve.reciprocal(inv[0:ROWS_OF_BATCH, :], den[0:ROWS_OF_BATCH, :]).then_inc(inverted, 1)

    return o, den, inv


def output_phase(nc, sem, ps, x, stats, woT, block_rows, sum_rows, sums_stored, o, den, inv, o_loaded,
                 inverted):
    spread = sem("op_spread")
    divided = sem("op_divided")
    projected = sem("op_projected")
    added = sem("op_added")
    SPREAD, OUT = 0, 2
    with ExitStack() as tmp:
        oT = tmp.enter_context(nc.sbuf_tensor("op_oT", [P, 2, BLK], F32))
        o_second = tmp.enter_context(nc.sbuf_tensor("op_o_second", [P, BPS, BLK], F32))
        block = tmp.enter_context(nc.Block())

        def rows(blk):
            b = blk // BPS
            return slice(b * ROWS_OF_BATCH, (b + 1) * ROWS_OF_BATCH)

        @block.sync
        def _(sp):
            sp.wait_ge(sums_stored, 16 * SUM_DMAS * BH + PRIME)
            load_sums(sp, 1, sum_rows, o_second, den, o_loaded[1])

        @block.vector
        def _(dve):
            for blk in range(NB + 1):
                if blk == BPS:
                    dve.wait_ge(o_loaded[1], 16 * (1 + BPS))
                    dve.reciprocal(inv[rows(blk), :], den[rows(blk), :]).then_inc(inverted, 1)
                if blk < NB:
                    dve.wait_ge(spread, blk + 1)
                    if blk >= 2:
                        dve.wait_ge(projected, blk - 1)
                    sums = (o, o_second)[blk // BPS][:, blk % BPS, :]
                    dve.tensor_tensor(oT[:, blk % 2, :], sums, ps[:, SPREAD + blk % 2, :], ALU.mult).then_inc(divided, 1)
                if blk >= 1:
                    n = blk - 1
                    dve.wait_ge(projected, n + 1)
                    tiles = x[:, n * TPB:(n + 1) * TPB, :].rearrange("p n d -> p (n d)")
                    dve.tensor_tensor(tiles, ps[:, OUT + n % 2, :], tiles, ALU.add).then_inc(added, 1)
                    dve.wait_ge(added, n + 1)
                    for j in range(n * TPB, (n + 1) * TPB):
                        dve.bn_stats(stats[:, j, :], x[:, j, :])

        @block.tensor
        def _(pe):
            for blk in range(NB + 1):
                if blk < NB:
                    pe.wait_ge(inverted, blk // BPS + 1)
                    if blk >= 2:
                        pe.wait_ge(divided, blk - 1)
                    pe.matmul(ps[:, SPREAD + blk % 2, :], block_rows[rows(blk), blk, :], inv[rows(blk), :],
                              start=True, stop=True).then_inc(spread, 1)
                if blk >= 1:
                    n = blk - 1
                    pe.wait_ge(divided, n + 1)
                    if n >= 2:
                        pe.wait_ge(added, n - 1)
                    for j in range(TPB):
                        last = pe.matmul(ps[:, OUT + n % 2, j * D:(j + 1) * D], oT[:, n % 2, j * P:(j + 1) * P], woT[:],
                                         start=True, stop=True)
                    last.then_inc(projected, 1)


_INS = ["L0_attn_x", "L0_attn_rope_cos", "L0_attn_rope_sin", "L0_attn_wq", "L0_attn_wk", "L0_attn_wv",
        "L0_attn_wo", "L0_attn_q_norm_w", "L0_attn_k_norm_w", "L0_ffn_gate_w", "L0_ffn_w_gate",
        "L0_ffn_w_up", "L0_ffn_w_down", "L0_ffn_sw_gate", "L0_ffn_sw_up", "L0_ffn_sw_down",
        "L0_ffn_shared_gate_w"]


def _constants():
    import numpy as np

    row = np.arange(P)
    col = np.arange(CH * P)
    expert = np.tile(np.arange(E + 1), 3)
    return {
        "ident": np.eye(P, dtype=np.float32),
        "expert_rows": (expert[:, None] == col[None, :] // I).astype(np.float32),
        "block_rows": np.stack([row[:, None] == (b * HEADS + row[None, :] // HD) * BPS + n
                                for b in range(BATCH) for n in range(BPS)], axis=1).astype(np.float32),
        "dim_rows": (np.arange(HD)[:, None] == row[None, :] % HD).astype(np.float32),
        "pair_rows": np.stack([
            (np.arange(HD // 2)[:, None] == row[None, :] % HD // 2).astype(np.float32),
            (np.arange(HD // 2)[:, None] == row[None, :] % HD // 2) * np.where(row % 2 == 0, -1, 1).astype(np.float32),
        ], axis=1).astype(np.float32),
        "head_mean": (row[:, None] // HD == np.arange(HEADS)[None, :]).astype(np.float32) / HD,
        "swap": (row[:, None] == (row[None, :] ^ 1)).astype(np.float32),
        "rank": np.tile(np.arange(E, 0, -1, dtype=np.float32), (P, 1)),
    }


def kernel(**inputs):
    import numpy as _np
    import concourse.bacc as _bacc
    from concourse import mybir as _mybir
    from concourse.bass_utils import run_bass_kernel_spmd as _run

    nc = _bacc.Bacc("TRN2", target_bir_lowering=False, num_devices=1)
    arrays, args = {}, []
    for name in _INS:
        a = _np.ascontiguousarray(inputs[name])
        arrays[f"in_{name}_dram"] = a
        args.append(nc.dram_tensor(f"in_{name}_dram", a.shape, _mybir.dt.from_np(a.dtype), kind="ExternalInput").ap())
    for name, a in _constants().items():
        arrays[f"const_{name}_dram"] = a
        args.append(nc.dram_tensor(f"const_{name}_dram", a.shape, _mybir.dt.from_np(a.dtype), kind="ExternalInput").ap())
    args.append(nc.dram_tensor("out_0_dram", (BATCH, SEQ, D), F32, kind="ExternalOutput").ap())
    build(nc, *args)
    r = _run(nc, [arrays], core_ids=[0])
    return r.results[0]["out_0_dram"]
```
